# Optimizing a Trainium2 kernel written in Bass

```python
import numpy as np
import jax
import jax.numpy as jnp

def _softmax(x, axis=-1):
    return jax.nn.softmax(x, axis=axis)

def _gelu(x):
    return jax.nn.gelu(x, approximate=True)

def _silu(x):
    return jax.nn.silu(x)

def _sigmoid(x):
    return jax.nn.sigmoid(x)

def _layernorm(x, axis=-1, eps=1e-05):
    m = jnp.mean(x, axis=axis, keepdims=True)
    v = jnp.var(x, axis=axis, keepdims=True)
    return (x - m) / jnp.sqrt(v + eps)

def _scatter_add(tgt, idx, src, axis=0):
    return tgt.at[idx].add(src)

def _segment_sum(src, seg, n):
    return jax.ops.segment_sum(src, seg, n)
kernel_name = 'mk_gnn_resnorm_d4_gnn_r8_da2587'

def setup_inputs(seed: int=0):
    np.random.seed(seed)
    _w = jnp.asarray

    def _rec_inputs():
        import jax
        import jax.numpy as jnp
        _gk = jax.random.key(seed)
        x = -0.0001538 + 1 * jax.random.normal(jax.random.fold_in(_gk, 1), (1536, 512), jnp.float32)
        _s = jax.random.randint(jax.random.fold_in(_gk, 2), (12288,), 0, 1536, jnp.int32)
        _d = jax.random.randint(jax.random.fold_in(_gk, 3), (12288,), 0, 1536, jnp.int32)
        _loop = jnp.arange(1536, dtype=jnp.int32)
        src = jnp.concatenate([_s, _d, _loop])
        dst = jnp.concatenate([_d, _s, _loop])
        _o = jnp.argsort(dst, stable=True)
        src = src[_o]
        dst = dst[_o]
        edge_type_2 = jax.random.randint(jax.random.fold_in(_gk, 14), (26112,), 0, 2, jnp.int32)
        edge_weight = jax.random.uniform(jax.random.fold_in(_gk, 15), (26112,), jnp.float32, 0.0, 0.999998)
        return (x, src, dst, edge_type_2, edge_weight)
    x, src, dst, edge_type_2, edge_weight = _rec_inputs()

    def _L0_gnn_setup():
        import jax, jax.numpy as jnp
        import numpy as np
        N = 1536
        B = 64
        R = 36
        E = 24576
        D_IN = 512
        D_OUT = 512
        P = 256
        D_IMG = 1024
        key = jax.random.key(seed)
        ks = jax.random.split(key, 12)

        def w(k, shape, fan_in):
            return jax.random.normal(k, shape, dtype=jnp.float32) / np.float32(np.sqrt(fan_in))
        return {'h': jax.random.normal(ks[0], (N, D_IN), dtype=jnp.float32), 'img_feats': jax.random.normal(ks[1], (B, R, D_IMG), dtype=jnp.float32), 'batch_ids': jax.random.randint(ks[2], (N,), 0, B, dtype=jnp.int32), 'src': jax.random.randint(ks[3], (E,), 0, N, dtype=jnp.int32), 'dst': jax.random.randint(ks[4], (E,), 0, N, dtype=jnp.int32), 'Wf': w(ks[5], (D_IN, P), D_IN), 'bf': jnp.zeros((P,), jnp.float32), 'Wi': w(ks[6], (D_IMG, P), D_IMG), 'bi': jnp.zeros((P,), jnp.float32), 'Wa': w(ks[7], (P, 1), P), 'ba': jnp.zeros((1,), jnp.float32), 'Wn': w(ks[8], (D_IN, D_OUT), D_IN), 'bn': jnp.zeros((D_OUT,), jnp.float32), 'Wim': w(ks[9], (D_IMG, D_OUT), D_IMG), 'bim': jnp.zeros((D_OUT,), jnp.float32), 'Wap': w(ks[10], (2 * D_OUT, D_OUT), 2 * D_OUT), 'bap': jnp.zeros((D_OUT,), jnp.float32)}
    _L0_gnn_all = _L0_gnn_setup()
    _L0_gnn_in = {k: v for k, v in _L0_gnn_all.items() if k in ('img_feats', 'Wf', 'bf', 'Wi', 'bi', 'Wa', 'ba', 'Wn', 'bn', 'Wim', 'bim', 'Wap', 'bap')}
    del _L0_gnn_all

    def _L1_gnn_setup():
        import jax, jax.numpy as jnp
        import numpy as np
        NUM_RELATIONS = 2
        NUM_BASES = 30
        HIDDEN = 512
        N_NODES = 1250
        N_EDGES = 20000

        def rgcn_gate_layer(x, row, col, edge_type, basis, att, gate_w, root, bias):
            H = x.shape[1]
            w = jnp.einsum('rb,bio->rio', att, basis)
            x_j = x[col]
            msgs = []
            for r in range(NUM_RELATIONS):
                gate = jax.nn.sigmoid(x_j @ gate_w[r, :, 0])
                msgs.append(gate[:, None] * x_j @ w[r])
            msg = jnp.where((edge_type == 0)[:, None], msgs[0], msgs[1])
            agg = jax.ops.segment_sum(msg, row, num_segments=x.shape[0])
            return agg + x @ root + bias
        key = jax.random.key(seed)
        ks = jax.random.split(key, 16)
        H, R, B = (HIDDEN, NUM_RELATIONS, NUM_BASES)
        bound = 1.0 / np.sqrt(B * H)
        u = lambda k, shape: jax.random.uniform(k, shape, jnp.float32, -bound, bound)
        inp = {'x': jax.random.normal(ks[0], (N_NODES, H), jnp.float32), 'edge_index': jax.random.randint(ks[1], (2, N_EDGES), 0, N_NODES, jnp.int32), 'edge_type': jax.random.randint(ks[2], (N_EDGES,), 0, R, jnp.int32), 'basis1': u(ks[3], (B, H, H)), 'att1': u(ks[4], (R, B)), 'gate_w1': u(ks[5], (R, H, 1)), 'root1': u(ks[6], (H, H)), 'bias1': u(ks[7], (H,)), 'basis2': u(ks[8], (B, H, H)), 'att2': u(ks[9], (R, B)), 'gate_w2': u(ks[10], (R, H, 1)), 'root2': u(ks[11], (H, H)), 'bias2': u(ks[12], (H,))}
        return inp
    _L1_gnn_all = _L1_gnn_setup()
    _L1_gnn_in = {k: v for k, v in _L1_gnn_all.items() if k in ('basis1', 'att1', 'gate_w1', 'root1', 'bias1', 'basis2', 'att2', 'gate_w2', 'root2', 'bias2')}
    del _L1_gnn_all

    def _L2_gnn_setup():
        import jax, jax.numpy as jnp
        import numpy as np
        N, E, F, H, L = (1250, 20000, 512, 512, 5)

        def _gin_layer(h, src, dst, W, b, e, num_nodes):
            agg = jax.ops.segment_sum(h[src], dst, num_segments=num_nodes)
            z = (1.0 + e) * h + agg
            return jax.nn.relu(z @ W + b)
        key = jax.random.key(seed)
        ks = jax.random.split(key, 6)
        x = jax.random.normal(ks[0], (N, F), dtype=jnp.float32)
        edge_index = jax.random.randint(ks[1], (2, E), 0, N, dtype=jnp.int64)
        W1 = jax.random.normal(ks[2], (F, H), dtype=jnp.float32) * (1.0 / np.sqrt(F))
        b1 = jnp.zeros((H,), dtype=jnp.float32)
        Ws = jax.random.normal(ks[3], (L - 1, H, H), dtype=jnp.float32) * (1.0 / np.sqrt(H))
        bs = jnp.zeros((L - 1, H), dtype=jnp.float32)
        eps = jnp.zeros((L,), dtype=jnp.float32)
        return {'x': x, 'edge_index': edge_index, 'W1': W1, 'b1': b1, 'Ws': Ws, 'bs': bs, 'eps': eps}
    _L2_gnn_all = _L2_gnn_setup()
    _L2_gnn_in = {k: v for k, v in _L2_gnn_all.items() if k in ('W1', 'b1', 'Ws', 'bs', 'eps')}
    del _L2_gnn_all

    def _L3_gnn_setup():
        import jax, jax.numpy as jnp
        import numpy as np
        N_NODES = 6250
        key = jax.random.key(seed)
        k1, k2, k3, k4, k5 = jax.random.split(key, 5)
        N, E, DIN, DOUT = (N_NODES, 200000, 512, 512)
        x = jax.random.normal(k1, (N, DIN), dtype=jnp.float32)
        weight = jax.random.normal(k2, (DIN, DOUT), dtype=jnp.float32) * (1.0 / np.sqrt(DIN))
        bias = jax.random.normal(k3, (DOUT,), dtype=jnp.float32) * 0.02
        edge_index = jax.random.randint(k4, (2, E), 0, N, dtype=jnp.int64)
        edge_vals = jax.random.uniform(k5, (E,), dtype=jnp.float32)
        return {'x': x, 'weight': weight, 'bias': bias, 'edge_index': edge_index, 'edge_vals': edge_vals}
    _L3_gnn_all = _L3_gnn_setup()
    _L3_gnn_in = {k: v for k, v in _L3_gnn_all.items() if k in ('weight', 'bias')}
    del _L3_gnn_all
    return {'x': x, 'src': src, 'dst': dst, 'edge_type_2': edge_type_2, 'edge_weight': edge_weight, 'L0_gnn_img_feats': _L0_gnn_in['img_feats'], 'L0_gnn_Wf': _L0_gnn_in['Wf'], 'L0_gnn_bf': _L0_gnn_in['bf'], 'L0_gnn_Wi': _L0_gnn_in['Wi'], 'L0_gnn_bi': _L0_gnn_in['bi'], 'L0_gnn_Wa': _L0_gnn_in['Wa'], 'L0_gnn_ba': _L0_gnn_in['ba'], 'L0_gnn_Wn': _L0_gnn_in['Wn'], 'L0_gnn_bn': _L0_gnn_in['bn'], 'L0_gnn_Wim': _L0_gnn_in['Wim'], 'L0_gnn_bim': _L0_gnn_in['bim'], 'L0_gnn_Wap': _L0_gnn_in['Wap'], 'L0_gnn_bap': _L0_gnn_in['bap'], 'L1_gnn_basis1': _L1_gnn_in['basis1'], 'L1_gnn_att1': _L1_gnn_in['att1'], 'L1_gnn_gate_w1': _L1_gnn_in['gate_w1'], 'L1_gnn_root1': _L1_gnn_in['root1'], 'L1_gnn_bias1': _L1_gnn_in['bias1'], 'L1_gnn_basis2': _L1_gnn_in['basis2'], 'L1_gnn_att2': _L1_gnn_in['att2'], 'L1_gnn_gate_w2': _L1_gnn_in['gate_w2'], 'L1_gnn_root2': _L1_gnn_in['root2'], 'L1_gnn_bias2': _L1_gnn_in['bias2'], 'L2_gnn_W1': _L2_gnn_in['W1'], 'L2_gnn_b1': _L2_gnn_in['b1'], 'L2_gnn_Ws': _L2_gnn_in['Ws'], 'L2_gnn_bs': _L2_gnn_in['bs'], 'L2_gnn_eps': _L2_gnn_in['eps'], 'L3_gnn_weight': _L3_gnn_in['weight'], 'L3_gnn_bias': _L3_gnn_in['bias']}

def reference(x, src, dst, edge_type_2, edge_weight, L0_gnn_img_feats, L0_gnn_Wf, L0_gnn_bf, L0_gnn_Wi, L0_gnn_bi, L0_gnn_Wa, L0_gnn_ba, L0_gnn_Wn, L0_gnn_bn, L0_gnn_Wim, L0_gnn_bim, L0_gnn_Wap, L0_gnn_bap, L1_gnn_basis1, L1_gnn_att1, L1_gnn_gate_w1, L1_gnn_root1, L1_gnn_bias1, L1_gnn_basis2, L1_gnn_att2, L1_gnn_gate_w2, L1_gnn_root2, L1_gnn_bias2, L2_gnn_W1, L2_gnn_b1, L2_gnn_Ws, L2_gnn_bs, L2_gnn_eps, L3_gnn_weight, L3_gnn_bias):
    import jax
    import jax.numpy as jnp

    def _L0_gnn_ref(h, img_feats, batch_ids, src, dst, Wf, bf, Wi, bi, Wa, ba, Wn, bn, Wim, bim, Wap, bap):
        import jax, jax.numpy as jnp
        import numpy as np
        N = 1536
        B = 64
        R = 36
        E = 24576
        D_IN = 512
        D_OUT = 512
        P = 256
        D_IMG = 1024
        node_proj = h @ Wf + bf
        img_proj = img_feats @ Wi + bi
        img_proj_n = img_proj[batch_ids]
        logits = (jnp.tanh(node_proj[:, None, :] + img_proj_n) @ Wa)[..., 0] + ba[0]
        att = jax.nn.softmax(logits, axis=1)
        img_n = img_feats[batch_ids]
        img = jnp.einsum('nr,nrd->nd', att, img_n)
        h1 = h @ Wn + bn
        neigh = jax.ops.segment_sum(h1[src], dst, num_segments=N)
        msg = neigh + img @ Wim + bim
        out = jax.nn.relu(jnp.concatenate([msg, h1], axis=1) @ Wap + bap)
        return out

    def _L1_gnn_ref(x, edge_index, edge_type, basis1, att1, gate_w1, root1, bias1, basis2, att2, gate_w2, root2, bias2):
        import jax, jax.numpy as jnp
        import numpy as np
        NUM_RELATIONS = 2
        NUM_BASES = 30
        HIDDEN = 512
        N_NODES = 1250
        N_EDGES = 20000

        def rgcn_gate_layer(x, row, col, edge_type, basis, att, gate_w, root, bias):
            H = x.shape[1]
            w = jnp.einsum('rb,bio->rio', att, basis)
            x_j = x[col]
            msgs = []
            for r in range(NUM_RELATIONS):
                gate = jax.nn.sigmoid(x_j @ gate_w[r, :, 0])
                msgs.append(gate[:, None] * x_j @ w[r])
            msg = jnp.where((edge_type == 0)[:, None], msgs[0], msgs[1])
            agg = jax.ops.segment_sum(msg, row, num_segments=x.shape[0])
            return agg + x @ root + bias
        row, col = (edge_index[0], edge_index[1])
        h = jax.nn.relu(rgcn_gate_layer(x, row, col, edge_type, basis1, att1, gate_w1, root1, bias1))
        out = rgcn_gate_layer(h, row, col, edge_type, basis2, att2, gate_w2, root2, bias2)
        return out

    def _L2_gnn_ref(x, edge_index, W1, b1, Ws, bs, eps):
        import jax, jax.numpy as jnp
        import numpy as np
        N, E, F, H, L = (1250, 20000, 512, 512, 5)

        def _gin_layer(h, src, dst, W, b, e, num_nodes):
            agg = jax.ops.segment_sum(h[src], dst, num_segments=num_nodes)
            z = (1.0 + e) * h + agg
            return jax.nn.relu(z @ W + b)
        src, dst = (edge_index[0], edge_index[1])
        num_nodes = x.shape[0]
        h = _gin_layer(x, src, dst, W1, b1, eps[0], num_nodes)
        for i in range(Ws.shape[0]):
            h = _gin_layer(h, src, dst, Ws[i], bs[i], eps[i + 1], num_nodes)
        return jax.nn.log_softmax(h, axis=1)

    def _L3_gnn_ref(x, weight, bias, edge_index, edge_vals):
        import jax, jax.numpy as jnp
        import numpy as np
        N_NODES = 6250
        support = x @ weight
        dst, src = (edge_index[0], edge_index[1])
        msgs = support[src] * edge_vals[:, None]
        out = jax.ops.segment_sum(msgs, dst, num_segments=x.shape[0])
        return out + bias
    edge_index = jnp.stack([src, dst])
    batch0 = jnp.zeros((1536,), jnp.int32)
    x = _layernorm(x + _L0_gnn_ref(x, L0_gnn_img_feats, batch0, src, dst, L0_gnn_Wf, L0_gnn_bf, L0_gnn_Wi, L0_gnn_bi, L0_gnn_Wa, L0_gnn_ba, L0_gnn_Wn, L0_gnn_bn, L0_gnn_Wim, L0_gnn_bim, L0_gnn_Wap, L0_gnn_bap), axis=-1)
    x = _layernorm(x + _L1_gnn_ref(x, edge_index, edge_type_2, L1_gnn_basis1, L1_gnn_att1, L1_gnn_gate_w1, L1_gnn_root1, L1_gnn_bias1, L1_gnn_basis2, L1_gnn_att2, L1_gnn_gate_w2, L1_gnn_root2, L1_gnn_bias2), axis=-1)
    x = _layernorm(x + _L2_gnn_ref(x, edge_index, L2_gnn_W1, L2_gnn_b1, L2_gnn_Ws, L2_gnn_bs, L2_gnn_eps), axis=-1)
    x = _layernorm(x + _L3_gnn_ref(x, L3_gnn_weight, L3_gnn_bias, edge_index, edge_weight), axis=-1)
    return x

_drawn_inputs = setup_inputs


def setup_inputs(seed=0):
    import zlib

    import numpy as np

    out = dict(_drawn_inputs(seed))
    spreads = {'L0_gnn_bf': (0.0, 2.0),
     'L0_gnn_bi': (0.0, 2.0),
     'L0_gnn_bn': (0.0, 0.1),
     'L0_gnn_bim': (0.0, 0.1),
     'L0_gnn_bap': (0.0, 0.1),
     'L2_gnn_b1': (0.0, 0.491),
     'L2_gnn_bs': (0.0, 2.0),
     'L2_gnn_eps': (0.0, 2.0)}
    factors = {'L0_gnn_Wf': 64.0,
     'L1_gnn_basis1': 8.0,
     'L1_gnn_att1': 8.0,
     'L1_gnn_gate_w1': 8.0,
     'L1_gnn_root1': 8.0,
     'L1_gnn_bias1': 8.0,
     'L1_gnn_basis2': 8.0,
     'L1_gnn_att2': 8.0,
     'L1_gnn_gate_w2': 8.0,
     'L1_gnn_root2': 4.991,
     'L1_gnn_bias2': 4.741,
     'L3_gnn_bias': 8.0,
     'L0_gnn_Wi': 8.0,
     'L0_gnn_Wa': 8.0}
    for name, (base, spread) in spreads.items():
        noise = np.random.default_rng([zlib.crc32(name.encode()), seed]).standard_normal(out[name].shape)
        drawn = base * np.exp(spread * noise) if base else spread * noise
        out[name] = jnp.asarray(drawn.astype(out[name].dtype))
    for name, factor in factors.items():
        out[name] = (out[name] * factor).astype(out[name].dtype)
    return out
```

```python
import concourse.bass as bass
from concourse import mybir
from contextlib import ExitStack

F32, F16, BF16 = mybir.dt.float32, mybir.dt.float16, mybir.dt.bfloat16
I32 = mybir.dt.int32
ALU, ACT, AX = mybir.AluOpType, mybir.ActivationFunctionType, mybir.AxisListType

P = 128
N, D = 1536, 512
NT = N // P
E = 26112
ET = E // P
ER = ET // 2
W = 16
NW = N // W
NPART = 6
V_OF = {1: 0, 3: 1, 4: 2, 5: 3, 6: 4, 7: 5}
NORM_OF = {0: 0, 2: 1, 7: 2, 8: 3}
R_OF = {n: r for r, n in NORM_OF.items()}
BB_COUNT = {3: 3, 4: 4, 5: 4, 6: 5, 7: 5, 8: 6}
MEASURED = (0, 2, 4, 5, 6, 7)
N_SMALL = 5 + 4 + 16
RG, PJ = 36, 256
FAR = 1000.0


def tick(r, i):
    return NT * r + i + 1


def program(nc, ins, out, debug=None, upto=9):
    with ExitStack() as ctx:
        def sb(name, shape, dt):
            return ctx.enter_context(nc.sbuf_tensor(name, shape, dt))

        def sem(name):
            return ctx.enter_context(nc.semaphore(name))

        adj = sb("adj", [P, 3, NT, N], F16)
        hs = sb("hs", [P, 2, 2, NT, D], F16)
        xt = sb("xt", [P, NT, 4, P], F32)
        ident = sb("ident", [P, P], F32)
        ident16 = sb("ident16", [P, P], F16)
        psum = ctx.enter_context(nc.psum_tensor("psum", [P, 8, 512], F32))
        hflat = hs[:, :, :, :, :].rearrange("p a b c d -> p (a b c d)")
        wb = sb("wb", [P, 2, 4, D], F32)
        ua = sb("ua", [P, 2, D], F32)
        vt = sb("vt", [P, D], F32)
        ones = sb("ones", [P, P], F32)
        img_t = sb("img_t", [P, 8, RG], F32)
        wa_pad = sb("wa_pad", [P, 2, 64], F32)
        pbias = sb("pbias", [P, 2, RG], F32)
        bcol = sb("bcol", [P, 8], F32)
        norm2 = sb("norm2", [P, NT], F32)
        att = sb("att", [P, 2, RG], F32)
        sml = sb("sml", [P, 2, 8], F32)
        lnst = sb("lnst", [P, 2, 12], F32)
        scl = sb("scl", [P, 8], F32)
        scl_i = sb("scl_i", [P, 2], I32)
        epsc = sb("epsc", [P, 8], F32)
        gates = sb("gates", [P, 2, 4], F32)
        gw = sb("gw", [P, 2, 4, 2], F32)
        attc = sb("attc", [P, 2, 2], F32)
        attm = sb("attm", [P, 4], F32)
        attw = sb("attw", [P, 2, 32], F32)

        def part(buf, byte, shape, dt=F32):
            n = 1
            for d in shape:
                n *= d
            v = buf[:, byte // 2:(byte + n * 4) // 2].bitcast(dt)
            if len(shape) == 1:
                return v
            names = "abcd"[:len(shape)]
            return v.rearrange(f"p ({' '.join(names)}) -> p {' '.join(names)}", **{k: n_ for k, n_ in zip(names, shape)})

        H1 = 2 * NT * D * 2
        proj = part(hflat, 0, [2, N])
        wi = part(hflat, 12288, [8, PJ])
        img = part(hflat, 12288 + 8192, [1024])
        tanh = part(hflat, H1, [4, N])
        logit_t = tanh[:, 3, :]
        att_t = part(hflat, H1, [N])
        g_sb = part(hflat, H1 + 6144, [D])
        wim = wb[:, :, :, :].rearrange("p a b n -> p (a b) n")
        wf = wb[:, 0, :, 0:PJ]
        adj_flat = [adj[:, m, :, :].rearrange("p j n -> p (j n)") for m in range(3)]
        base = {0: (hflat, H1 + 8192), 1: (adj_flat[0], 8192), 2: (hflat, H1)}
        kit_of = [0, 1, 1, 2, 2, 2, 2, 2, 2]
        kits = {}
        for k, (buf, at0) in base.items():
            kits[k] = dict(xin=part(buf, at0, [2, D]), bb=part(buf, at0 + 4096, [2, D]),
                           mt=part(buf, at0 + 8192, [2, 4, P]), yb=part(buf, at0 + 12288, [2, D]))
        root = part(adj_flat[0], 0, [4, D])
        sup = part(hflat, 0, [NT, D])
        aw = part(adj[:, 1:3, :, :].rearrange("p m j n -> p (m j n)"), 0, [NT, N])
        basis = part(adj_flat[0], 0, [4, 4 * D])
        comb = part(hflat, 0, [2, 8, D])
        xs_dram = [nc.dram_tensor(f"x{k}_scratch", [N, D], F32, kind="Internal").ap() for k in range(3)]
        as_dram = nc.dram_tensor("as_scratch", [P, NT * N], F16, kind="Internal").ap()
        wc_dram = [nc.dram_tensor(f"comb{k}_scratch", [8, P, D], F32, kind="Internal").ap() for k in range(2)]
        aw_dram = nc.dram_tensor("aw_scratch", [P, NT, N], F32, kind="Internal").ap()

        flat = hs[:, :, :, :, :].rearrange("p a b c d -> p (a b c d)")
        at = 0

        def lay(n, dt, shape_str=None, **kw):
            nonlocal at
            size = n * (2 if dt in (F16, BF16) else 4) // 2
            v = flat[:, at:at + size]
            at += size
            if dt != F16:
                v = v.bitcast(dt)
            return v.rearrange(shape_str, **kw) if shape_str else v

        erow_i = lay(4 * 256, I32, "p (a e) -> p a e", a=4)
        erow = lay(4 * 256, F32, "p (a e) -> p a e", a=4)
        ecol = lay(4 * 206, F32, "p (a t) -> p a t", a=4)
        wrem = lay(2 * 206, F32, "p (a t) -> p a t", a=2)
        vals = lay(208 * NPART, BF16, "p (t v) -> p t v", v=NPART)
        iota_s = lay(N, F16)
        iota_d = lay(N, F32)
        onehot_s = lay(2 * N, F16, "p (k s) -> p k s", k=2)
        onehot_d = lay(2 * NPART * W, BF16, "p (k v w) -> p k v w", k=2, v=NPART)
        aw_stage = xt[:, :, :, :].rearrange("p a b d -> p (a b d)")[:, 0:2 * NT * P].rearrange("p (k j d) -> p k j d", k=2, j=NT)
        span = lay(2 * 2 * NW, F32, "p (f h w) -> p f h w", f=2, h=2)
        spant = lay(2 * NW, F32, "p (h w) -> p h w", h=2)
        trange = lay(4, F32)
        win16 = lay(NW, F32)
        tileno = lay(4, F32)
        wcol = lay(8, F32)
        wrow = lay(4 * NW, F32, "p (a w) -> p a w", a=4)
        wrow_i = lay(4 * NW, I32, "p (a w) -> p a w", a=4)
        zeros = lay(P, BF16)
        rest = xt[:, 6:8, :, :].rearrange("p a b d -> p (a b d)")
        rest = xt[:, :, :, :].rearrange("p a b d -> p (a b d)")[:, 2 * NT * P:]
        wparts = rest[:, 0:2 * NT * 3 * W].rearrange("p (k j c) -> p k j c", k=2, j=NT)
        wsum = rest[:, 2 * NT * 3 * W:2 * NT * 4 * W].rearrange("p (k j c) -> p k j c", k=2, j=NT)
        aw_row = rest[:, 2 * NT * 4 * W:2 * NT * 4 * W + N]
        typed = wb[:, :, :, :].rearrange("p a b n -> p (a b n)").bitcast(F16)[:, 0:2 * 2 * NT * P].rearrange("p (k m j d) -> p k m j d", k=2, m=2, j=NT)
        assert at <= 2 * 2 * NT * D

        c_ready = sem("c_ready")
        edges_in = sem("edges_in")
        erow_ready = sem("erow_ready")
        ecol_ps = sem("ecol_ps")
        span_ready = sem("span_ready")
        spant_ps = sem("spant_ps")
        wcol_ready = sem("wcol_ready")
        wrow_ps = sem("wrow_ps")
        ranges_ready = sem("ranges_ready")
        onehot_ready = [sem(f"onehot_ready{k}") for k in range(2)]
        onehot_free = [sem(f"onehot_free{k}") for k in range(2)]
        win_free = [sem(f"win_free{b}") for b in range(2)]
        wparts_free = [sem(f"wparts_free{b}") for b in range(2)]
        wsum_ready = [sem(f"wsum_ready{b}") for b in range(2)]
        turn_ps, turned_out, row_out = sem("turn_ps"), sem("turned_out"), sem("row_out")
        dve_done = sem("dve_done")

        built = sem("built")
        weights = {k: sem("in_" + k) for k in ("wf", "wi", "img", "wim", "small", "wn", "wt", "wbm", "l1a", "l1b", "aw", "as_out", "as_in")}
        gin_in = [sem(f"gin_in{k}") for k in range(6)]
        bias_in = {}
        x_in = [sem(f"x_in{k}") for k in range(2)]
        tiny = sem("tiny_ready")
        x_ps, x_cp, x_sq = sem("x_ps"), sem("x_cp"), sem("x_sq")
        proj_ps, proj_cp = sem("proj_ps"), sem("proj_cp")
        imgt_ps, imgt_cp, ip_ps, pb_ready = sem("imgt_ps"), sem("imgt_cp"), sem("ip_ps"), sem("pbias_ready")
        tanh_ready, tanh_used = sem("tanh_ready"), sem("tanh_used")
        lt_ready, ln_ps, sm_neg, sm_exp, att_ready, att_ps, att_cp = [sem(x) for x in (
            "logit_t_ready", "logit_ps", "negmax_ready", "exp_ready", "att_ready", "att_ps", "att_t_ready")]
        g_ps, g_ready = sem("g_ps"), sem("g_ready")
        sq_ready, sq_used, c2_ps = sem("sq_ready"), sem("sq_used"), sem("colnorm_ps")
        r2_col, r2_all, scale_ready = sem("rownorm_col"), sem("rownorm_all"), sem("scale_ready")
        u_ps, u_hi, u_lo = sem("u_ps"), sem("u_hi"), sem("u_lo")
        h1_ready, h1t_ps, h1t_cp = sem("h1_ready"), sem("h1t_ps"), sem("h1t_cp")
        acc_ps, acc_read = sem("acc_ps"), sem("acc_read")
        m_ps, m_cp = sem("m_ps"), sem("m_cp")
        o_ps, o_read = sem("o_ps"), sem("o_read")
        v_pre, v_ready = sem("v_pre"), sem("v_ready")
        t_ps, t_cp = sem("t_ps"), sem("t_cp")
        var_ready, std_ready = sem("var_ready"), sem("std_ready")
        y_ready, y_out = sem("y_ready"), [sem(f"y_out{k}") for k in range(2)]
        res_in = [sem(f"res_in{k}") for k in range(2)]
        gate_ps, gate_sig, gate_ready = sem("gate_ps"), sem("gate_sig"), sem("gate_ready")
        lsm_neg, lsm_exp = sem("lsm_negmax"), sem("lsm_lnsum")
        basis_in = [sem(f"basis_in{k}") for k in range(4)]
        comb_ps, comb_cp = sem("comb_ps"), sem("comb_cp")
        comb_out = [sem(f"comb_out{k}") for k in range(2)]
        act_done = sem("act_done")
        attw_ready = sem("attw_ready")
        bb_in = [sem(f"bb_in{k}") for k in range(2)]
        fin = sem("fin")

        block = ctx.enter_context(nc.Block())
        GB = 16
        win = [psum[:, 3 * b:3 * b + 3, :].rearrange("p k c -> p (k c)").rearrange("p (j c) -> p j c", j=NT)
               for b in range(2)]

        typed_ps = [psum[:, 6 + b, :].bitcast(F16) for b in range(2)]

        @block.sync
        def _(sp):
            for a, name in enumerate(("src", "dst", "edge_type_2")):
                sp.dma_start(erow_i[0:ER, a, :], ins[name].rearrange("(r e) -> r e", e=256)).then_inc(edges_in, 16)
            sp.dma_start(erow[0:ER, 3, :], ins["edge_weight"].rearrange("(r e) -> r e", e=256)).then_inc(edges_in, 16)
            with sp.Fori(0, NW // GB) as g:
                for s in range(2):
                    sp.wait_ge(turned_out, 6 * (2 * g + s + 1) + 2)
                    sp.dma_start(aw_dram[:, bass.ds(g * 2 + s, 1), :].rearrange("p o n -> p (o n)"), aw_row).then_inc(row_out, 16)
            sp.wait_ge(row_out, 16 * (NT + 1))

            sp.wait_ge(built, 4)
            sp.dma_start(as_dram, adj_flat[0]).then_inc(weights["as_out"], 16)
            sp.dma_start(wf, ins["L0_gnn_Wf"].rearrange("(k p) n -> p k n", p=P)).then_inc(weights["wf"], 16)
            sp.dma_start(wi, ins["L0_gnn_Wi"].rearrange("(k p) n -> p k n", p=P)).then_inc(weights["wi"], 16)
            sp.dma_start(img[0:RG, :], ins["L0_gnn_img_feats"][0]).then_inc(weights["img"], 16)
            small = [
                (bcol[:, 0:2], ins["L0_gnn_bf"].rearrange("(k p) -> p k", p=P)),
                (bcol[:, 2:4], ins["L0_gnn_bi"].rearrange("(k p) -> p k", p=P)),
                (bcol[:, 4:5], ins["L0_gnn_ba"].unsqueeze(0).broadcast_to([P, 1])),
                (wa_pad[:, :, 31:32], ins["L0_gnn_Wa"].rearrange("(k p) o -> p k o", p=P)),
                (epsc[:, 0:5], ins["L2_gnn_eps"].unsqueeze(0).broadcast_to([P, 5])),
            ]
            for l in range(2):
                for t in range(2):
                    small.append((gw[:, l, :, t], ins[f"L1_gnn_gate_w{l + 1}"][t].rearrange("(k p) o -> p (k o)", p=P)))
                    for j in range(4):
                        small.append((attc[j:120:4, l, t:t + 1], ins[f"L1_gnn_att{l + 1}"][t].unsqueeze(1)))
            for to, of in small:
                sp.dma_start(to, of, allow_slow_non_contiguous=True).then_inc(weights["small"], 16)
            assert len(small) == N_SMALL

            def x_tile(src, i):
                return src[P * i:P * i + P, :]

            for i in range(NT):
                if i >= 2:
                    sp.wait_ge(x_ps, i - 1)
                    sp.wait_ge(x_sq, i - 1)
                sp.dma_start(kits[0]["xin"][:, i % 2, :], x_tile(ins["x"], i)).then_inc(x_in[i % 2], 16)
            sp.wait_ge(proj_ps, 6)
            sp.dma_start(wim, ins["L0_gnn_Wim"].rearrange("(k p) n -> p k n", p=P)).then_inc(weights["wim"], 16)
            sp.wait_ge(g_ps, 1)
            wap = ins["L0_gnn_Wap"].rearrange("(h k p) n -> h p k n", h=2, p=P)
            sp.dma_start(wb[:, 0, :, :], ins["L0_gnn_Wn"].rearrange("(k p) n -> p k n", p=P)).then_inc(weights["wn"], 16)
            sp.dma_start(wb[:, 1, :, :], wap[0]).then_inc(weights["wt"], 16)
            sp.wait_ge(tanh_used, 72)
            sp.wait_ge(ln_ps, 3)
            biases = ["L0_gnn_bn", "L0_gnn_bim", "L0_gnn_bap"]

            def bias(slot, k, of):
                sp.dma_start(kits[k]["bb"][:, slot, :], of.unsqueeze(0).broadcast_to([P, D])).then_inc(bb_in[slot], 16)

            bias(0, 0, ins["L0_gnn_bn"])
            bias(1, 0, ins["L0_gnn_bim"])
            sp.wait_ge(u_ps, tick(0, NT - 1))
            sp.dma_start(wb[:, 0, :, :], wap[1]).then_inc(weights["wbm"], 16)
            sp.wait_ge(h1_ready, NT)
            bias(0, 0, ins["L0_gnn_bap"])

            def norm_tiles(n, k, src, dst):
                for i in range(NT + 1):
                    if i < NT:
                        if i >= 2:
                            sp.wait_ge(var_ready, tick(n, i - 2))
                        sp.dma_start(kits[k]["xin"][:, i % 2, :], x_tile(src, i)).then_inc(res_in[i % 2], 16)
                    if i > 0:
                        sp.wait_ge(y_ready, tick(n, i - 1))
                        sp.dma_start(x_tile(dst, i - 1), kits[k]["yb"][:, (i - 1) % 2, :]).then_inc(y_out[(i - 1) % 2], 16)

            if upto >= 1:
                norm_tiles(0, 0, ins["x"], xs_dram[0])
            if upto >= 2:
                sp.wait_ge(acc_ps, tick(0, NT - 1))
                sp.wait_ge(weights["as_out"], 16)
                for l in range(2):
                    flat_b = ins[f"L1_gnn_basis{l + 1}"].rearrange("b (j i) o -> (b j) (i o)", j=4)
                    for c in range(33):
                        cc = 32 * l + c
                        if c < 32:
                            if cc >= 4:
                                sp.wait_ge(comb_ps, cc - 3)
                            sp.dma_start(basis[0:120, cc % 4, :], flat_b[:, 4 * D * c:4 * D * (c + 1)]).then_inc(basis_in[cc % 4], 16)
                        if c % 8 == 0 and c:
                            o = 4 * l + c // 8 - 1
                            sp.wait_ge(comb_cp, 8 * (o + 1))
                            for q in range(4):
                                v = wc_dram[l].rearrange("j (c q) o -> q j c o", q=4)
                                sp.dma_start(v[q, :, c - 8:c, :], comb[32 * q:32 * q + 8, o % 2, :, :]).then_inc(comb_out[o % 2], 16)
            if upto >= 3:
                for k in range(2):
                    sp.wait_ge(comb_out[k], 16 * 4 * 4)
                for l in range(2):
                    r = 1 + l
                    if l:
                        sp.wait_ge(acc_ps, tick(1, NT - 1))
                        sp.wait_ge(o_ps, tick(1, NT - 1))
                    name = f"l1{'ab'[l]}"
                    for t in range(2):
                        sp.dma_start(wb[:, t, :, :], wc_dram[l][4 * t:4 * t + 4].rearrange("j p o -> p j o")).then_inc(weights[name], 16)
                    sp.dma_start(root, ins[f"L1_gnn_root{l + 1}"].rearrange("(k p) n -> p k n", p=P)).then_inc(weights[name], 16)
                    if l:
                        sp.wait_ge(o_read, tick(1, NT - 1))
                    bias(l, 1, ins[f"L1_gnn_bias{l + 1}"])
                norm_tiles(1, 1, xs_dram[0], xs_dram[1])
            if upto >= 4:
                sp.wait_ge(acc_ps, tick(2, NT - 1))
                for k in range(2):
                    sp.wait_ge(y_out[k], 16 * 12)
                sp.wait_ge(t_ps, tick(2, NT - 1))
                sp.wait_ge(y_ready, tick(1, NT - 1))
                sp.dma_start(adj_flat[0], as_dram).then_inc(weights["as_in"], 16)
                sp.dma_start(aw, aw_dram).then_inc(weights["aw"], 16)
                for l in range(5):
                    r = 3 + l
                    if l >= 2:
                        sp.wait_ge(u_ps, tick(r - 2, NT - 1))
                        sp.wait_ge(v_pre, tick(V_OF[r - 2] - 1, NT - 1))
                    w_in = ins["L2_gnn_W1"] if l == 0 else ins["L2_gnn_Ws"][l - 1]
                    b_in = ins["L2_gnn_b1"] if l == 0 else ins["L2_gnn_bs"][l - 1]
                    sp.dma_start(wb[:, r % 2, :, :], w_in.rearrange("(k p) n -> p k n", p=P)).then_inc(gin_in[l], 16)
                    bias(r % 2, 2, b_in)
                norm_tiles(2, 2, xs_dram[1], xs_dram[2])
            if upto >= 5:
                sp.dma_start(wb[:, 0, :, :], ins["L3_gnn_weight"].rearrange("(k p) n -> p k n", p=P)).then_inc(gin_in[5], 16)
                bias(0, 2, ins["L3_gnn_bias"])
                norm_tiles(3, 2, xs_dram[2], out)
            for k in range(2):
                sp.wait_ge(y_out[k], 16 * 6 * {1: 1, 2: 1, 3: 2, 4: 3, 5: 4}[min(upto, 5)])


        @block.gpsimd
        def _(pool):
            pool.memset(ident[:], 0.0).then_inc(c_ready, 1)
            pool.wait_ge(c_ready, 1)
            pool.affine_select(out=ident[:], in_=ident[:], compare_op=ALU.not_equal, fill=1.0, base=0,
                               pattern=[[-1, P]], channel_multiplier=1).then_inc(c_ready, 1)
            pool.wait_ge(c_ready, 2)
            pool.tensor_copy(ident16[:], ident[:])
            pool.memset(zeros, 0.0)
            pool.memset(ones[:], 1.0)
            pool.memset(wa_pad[:], 0.0)
            pool.memset(attw[:], 0.0)
            pool.memset(bcol[:, 5:6], 1e-5).then_inc(c_ready, 1)
            pool.iota(iota_s, [[1, N]], base=0, channel_multiplier=0,
                      allow_small_or_imprecise_dtypes=True).then_inc(c_ready, 1)
            pool.iota(iota_d, [[1, N]], base=0, channel_multiplier=0,
                      allow_small_or_imprecise_dtypes=True).then_inc(c_ready, 1)
            pool.iota(win16, [[W, NW]], base=0, channel_multiplier=0,
                      allow_small_or_imprecise_dtypes=True).then_inc(c_ready, 1)
            pool.iota(tileno[:, 0:2], [[1, 2]], base=1, channel_multiplier=2,
                      allow_small_or_imprecise_dtypes=True).then_inc(c_ready, 1)
            pool.iota(tileno[:, 2:4], [[-1, 2]], base=int(FAR), channel_multiplier=-2,
                      allow_small_or_imprecise_dtypes=True).then_inc(c_ready, 1)
            for k in range(2):
                pool.sem_inc(onehot_free[k], 1)
                pool.sem_inc(win_free[k], 1)
                pool.sem_inc(wparts_free[k], 1)
            pool.sem_inc(row_out, 16)
            pool.sem_inc(turned_out, 2)
            pool.sem_inc(turn_ps, 12)
            with pool.Fori(0, NW // GB) as g:
                for u in range(GB):
                    b, s = u % 2, u // 8
                    if u % 8 == 0:
                        pool.wait_ge(turn_ps, 12 * g + 6 * s + 6)
                    pool.wait_ge(win_free[b], (GB // 2) * g + u // 2 + 2)
                    part = [wparts[:, b, :, W * v:W * v + W] for v in range(3)]
                    pool.tensor_tensor(wsum[:, b, :, :], part[0], part[1], ALU.add).then_inc(wsum_ready[b], 1)
                    pool.wait_ge(wsum_ready[b], (GB // 2) * g + u // 2 + 1)
                    pool.tensor_tensor(aw_stage[:, s, :, W * (u % 8):W * (u % 8) + W],
                                       wsum[:, b, :, :], part[2], ALU.add).then_inc(wparts_free[b], 1)

            pool.drain().then_inc(built, 1)

            n_all = 0
            last_round = {0: -1, 1: 0, 2: 0, 3: 2, 4: 7}.get(upto, 8)
            for r in [0, 2, 3, 4, 5, 6, 7, 8]:
                if r in MEASURED and r <= last_round:
                    n_all += 1
                    pool.wait_ge(r2_col, n_all)
                    pool.partition_all_reduce(scl[:, 5:6], scl[:, 4:5], P, bass.bass_isa.ReduceOp.max).then_inc(r2_all, 1)

        @block.vector
        def _(dve):
            n_dve = [0]

            def step(ins_):
                n_dve[0] += 1
                ins_.then_inc(dve_done, 1)
                dve.wait_ge(dve_done, n_dve[0])

            dve.wait_ge(c_ready, 8)
            dve.wait_ge(edges_in, 64)
            dve.tensor_copy(erow[0:ER, 0:3, :], erow_i[0:ER, 0:3, :]).then_inc(erow_ready, 1)
            dve.wait_ge(erow_ready, 1)
            dst2 = erow[0:ER, 1, :].rearrange("p (h e) -> p h e", h=2)
            dve.tensor_reduce(trange[0:ER, 0:2], dst2, AX.X, ALU.min)
            step(dve.tensor_reduce(trange[0:ER, 2:4], dst2, AX.X, ALU.max))
            step(dve.tensor_scalar(trange[0:ER, 0:2], trange[0:ER, 0:2], float(-W), None, ALU.add))
            for h in range(2):
                dve.tensor_scalar(spant[0:ER, h, :], win16[0:ER, :], trange[0:ER, h:h + 1], None, ALU.is_gt)
            step(dve.tensor_copy(wcol[0:ER, 0:1], tileno[0:ER, 0:1]))
            for h in range(2):
                x = dve.scalar_tensor_tensor(spant[0:ER, h, :], win16[0:ER, :], trange[0:ER, 2 + h:3 + h],
                                         spant[0:ER, h, :], ALU.is_le, ALU.mult)
            step(x)
            for f in range(2):
                for h in range(2):
                    k = 2 * (1 - f) + h
                    x = dve.tensor_scalar(span[0:ER, f, h, :], spant[0:ER, h, :], tileno[0:ER, k:k + 1], None, ALU.mult)
                    x.then_inc(span_ready, 1)
            dve.memset(ecol[:, :, ET:206], -1.0)
            dve.wait_ge(ecol_ps, 1)
            for a in range(4):
                v = psum[:, a // 2, 256 * (a % 2):256 * (a % 2) + 2 * ER].rearrange("p (h r) -> p h r", h=2)
                x = dve.tensor_copy(ecol[:, a, 0:ET].rearrange("p (r h) -> p h r", h=2), v)
            step(x)
            dve.memset(vals[:, :, 0:1], 1.0)
            dve.tensor_scalar(vals[:, 0:206, 1], ecol[:, 2, :], 0.0, None, ALU.is_equal)
            dve.tensor_scalar(vals[:, 0:206, 2], ecol[:, 2, :], 0.0, None, ALU.not_equal)
            step(dve.tensor_copy(vals[:, 0:206, 3], ecol[:, 3, :]))
            step(dve.tensor_tensor(wrem[:, 0, :], ecol[:, 3, :], vals[:, 0:206, 3], ALU.subtract))
            step(dve.tensor_copy(vals[:, 0:206, 4], wrem[:, 0, :]))
            step(dve.tensor_tensor(vals[:, 0:206, 5], wrem[:, 0, :], vals[:, 0:206, 4], ALU.subtract))
            dve.wait_ge(spant_ps, 1)
            for f in range(2):
                v = psum[0:NW, 2 + f, 0:2 * ER]
                x = dve.tensor_reduce(wcol[0:NW, f:f + 1], v, AX.X, ALU.max)
            step(x)
            step(dve.tensor_scalar(wcol[0:NW, 2:3], wcol[0:NW, 0:1], -1.0, FAR, ALU.mult, ALU.add))
            step(dve.tensor_scalar(wcol[0:NW, 2:3], wcol[0:NW, 2:3], float(ET - 1), None, ALU.min))
            step(dve.tensor_tensor(wcol[0:NW, 3:4], wcol[0:NW, 1:2], wcol[0:NW, 2:3], ALU.subtract))
            step(dve.tensor_scalar(wcol[0:NW, 3:4], wcol[0:NW, 3:4], 1.0, 2.0, ALU.add, ALU.max))
            dve.tensor_scalar(wcol[0:NW, 3:4], wcol[0:NW, 3:4], 0.5, -0.25, ALU.mult, ALU.add).then_inc(wcol_ready, 1)
            dve.wait_ge(wrow_ps, 1)
            v = psum[0:1, 4, 0:2 * NW].rearrange("p (a w) -> p a w", a=2)
            step(dve.tensor_copy(wrow_i[0:1, 0:2, :], v))
            step(dve.tensor_copy(wrow[0:1, 0:2, :], wrow_i[0:1, 0:2, :]))
            step(dve.tensor_tensor_scan(wrow[0:1, 2, :], wrow[0:1, 1, :], wrow[0:1, 1, :], 0.0, ALU.add, ALU.bypass))
            step(dve.tensor_tensor(wrow[0:1, 3, :], wrow[0:1, 2, :], wrow[0:1, 1, :], ALU.subtract))
            dve.tensor_copy(wrow_i[0:1, 2:4, :], wrow[0:1, 2:4, :]).then_inc(ranges_ready, 1)
            dve.wait_ge(ranges_ready, 1)

            with dve.Fori(0, NW // GB) as g:
                for u in range(GB):
                    w = g * GB + u
                    first = dve.value_load(wrow_i[0:1, 0, bass.ds(w, 1)], min_val=0, max_val=ET - 1)
                    pairs = dve.value_load(wrow_i[0:1, 1, bass.ds(w, 1)], min_val=1, max_val=ER)
                    before = dve.value_load(wrow_i[0:1, 3, bass.ds(w, 1)], min_val=0, max_val=NW * ER)
                    with dve.Fori(0, pairs) as q:
                        for k in range(2):
                            t = nc.s_assert_within(first + 2 * q + k, 0, ET, skip_runtime_bounds_check_because="a window's pairs end with its last tile, or one past it")
                            dve.wait_ge(onehot_free[k], before + q + 1)
                            dve.tensor_scalar(onehot_s[:, k, :], iota_s, ecol[:, 0, bass.ds(t, 1)], None, ALU.is_equal)
                            dve.scalar_tensor_tensor(
                                onehot_d[:, k, :, :], iota_d[:, bass.ds(w * W, W)].unsqueeze(1).broadcast_to([P, NPART, W]),
                                ecol[:, 1, bass.ds(t, 1)], vals[:, bass.ds(t, 1), :].rearrange("p o v -> p (o v)").unsqueeze(2).broadcast_to([P, NPART, W]),
                                ALU.is_equal, ALU.mult).then_inc(onehot_ready[k], 1)
            dve.drain().then_inc(built, 1)

            dve.wait_ge(built, 4)
            dve.wait_ge(weights["small"], 16 * N_SMALL)
            step(dve.tensor_reduce(attm[0:120, :], ident[0:120, 0:120].rearrange("p (b j) -> p j b", j=4), AX.X, ALU.add))
            for l in range(2):
                for t in range(2):
                    x = dve.tensor_scalar(attw[0:120, l, 4 * t:4 * t + 4], attm[0:120, :], attc[0:120, l, t:t + 1], None, ALU.mult)
                x.then_inc(attw_ready, 1)
            dve.wait_ge(imgt_ps, 1)
            dve.tensor_copy(img_t[:, :, :].rearrange("p k r -> p (k r)"), psum[:, 4, 0:8 * RG]).then_inc(imgt_cp, 1)
            dve.wait_ge(ip_ps, 1)
            for h in range(2):
                x = dve.tensor_scalar(pbias[:, h, :], psum[:, 5, RG * h:RG * h + RG], bcol[:, 2 + h:3 + h], bcol[:, h:h + 1], ALU.add, ALU.add)
            x.then_inc(pb_ready, 1)
            for q in range(6):
                h, c = q % 2, q // 2
                dve.wait_ge(proj_ps, q + 1)
                dve.tensor_copy(proj[:, h, 512 * c:512 * c + 512], psum[:, 6 + q % 2, :]).then_inc(proj_cp, 1)
            dve.wait_ge(tanh_used, 72)
            for c in range(3):
                dve.tensor_scalar(logit_t[:, 512 * c:512 * c + 512], psum[:, c, :], bcol[:, 4:5], None, ALU.add).then_inc(lt_ready, 1)
            for i in range(NT + 1):
                if i < NT:
                    q, k = i // 4, i % 4
                    dve.wait_ge(ln_ps, q + 1)
                    if i >= 2:
                        dve.wait_ge(att_ready, i - 1)
                    v = psum[:, 4 + q, P * k:P * k + P].rearrange("p (g c) -> p g c", g=4)[:, :, 0:9]
                    dve.tensor_reduce(sml[:, i % 2, 0:1], v, AX.XY, ALU.max, negate=True).then_inc(sm_neg, 1)
                    dve.wait_ge(sm_exp, i + 1)
                    step(dve.reciprocal(sml[:, i % 2, 2:3], sml[:, i % 2, 1:2]))
                    dve.tensor_scalar(att[:, i % 2, :], att[:, i % 2, :], sml[:, i % 2, 2:3], None, ALU.mult).then_inc(att_ready, 1)
                if i:
                    dve.wait_ge(att_ps, i)
                    dve.tensor_copy(att_t[0:RG, P * (i - 1):P * i], psum[0:RG, (i - 1) % 2, 0:P]).then_inc(att_cp, 1)

            seen = [0]

            def scale(n_slots, bound2=None, bias_ap=None):
                if bound2 is None:
                    dve.tensor_reduce(scl[:, 4:5], norm2[:], AX.X, ALU.max).then_inc(r2_col, 1)
                seen[0] += 4 * n_slots
                dve.wait_ge(sq_used, seen[0])
                step(dve.tensor_reduce(scl[:, 6:7], psum[:, 0:n_slots, :].rearrange("p b c -> p (b c)"), AX.X, ALU.max))
                if bound2 is None:
                    n_r2[0] += 1
                    dve.wait_ge(r2_all, n_r2[0])
                    step(dve.tensor_scalar(scl[:, 6:7], scl[:, 6:7], scl[:, 5:6], 4.0, ALU.mult, ALU.mult))
                else:
                    step(dve.tensor_scalar(scl[:, 6:7], scl[:, 6:7], float(bound2), None, ALU.mult))
                if bias_ap is not None:
                    step(dve.tensor_reduce(scl[:, 7:8], bias_ap, AX.X, ALU.max, apply_absolute_value=True))
                    step(dve.tensor_scalar(scl[:, 7:8], scl[:, 7:8], scl[:, 7:8], 4.0, ALU.mult, ALU.mult))
                    step(dve.tensor_tensor(scl[:, 6:7], scl[:, 6:7], scl[:, 7:8], ALU.add))
                step(dve.tensor_scalar(scl[:, 6:7], scl[:, 6:7], 1e-30, 1e30, ALU.max, ALU.min))
                step(dve.tensor_scalar(scl_i[:, 0:1], scl[:, 6:7].bitcast(I32), 23, None, ALU.logical_shift_right))
                step(dve.tensor_scalar(scl_i[:, 0:1], scl_i[:, 0:1], 1.0, None, ALU.add))
                step(dve.tensor_scalar(scl_i[:, 0:1], scl_i[:, 0:1], 1, None, ALU.logical_shift_right))
                step(dve.tensor_scalar(scl_i[:, 1:2], scl_i[:, 0:1], 49.0, None, ALU.add))
                step(dve.tensor_scalar(scl_i[:, 0:1], scl_i[:, 0:1], -1.0, 205.0, ALU.mult, ALU.add))
                dve.tensor_scalar(scl[:, 0:2].bitcast(I32), scl_i[:, 0:2], 23, None, ALU.logical_shift_left).then_inc(scale_ready, 1)
                n_scale[0] += 1
                dve.wait_ge(scale_ready, n_scale[0])

            n_r2, n_scale = [0], [0]

            def norm_end(n, i, k, st, y):
                kit = kits[k]
                dve.wait_ge(std_ready, tick(n, i))
                step(dve.reciprocal(st[:, 9:10], st[:, 8:9]))
                if tick(n, i) > 2:
                    t = NT * n + i
                    dve.wait_ge(y_out[i % 2], 16 * (t // 2))
                if n < 3 and i >= 2:
                    dve.wait_ge(t_ps, tick(R_OF[n], i - 2))
                dve.tensor_scalar(kit["yb"][:, i % 2, :], y, st[:, 6:7], st[:, 9:10], ALU.subtract, ALU.mult).then_inc(y_ready, 1)
                dve.wait_ge(y_ready, tick(n, i))

            dve.wait_ge(weights["wn"], 16)
            dve.wait_ge(x_sq, NT)
            dve.wait_ge(bb_in[0], 16)
            kit = kits[0]
            scale(1, None, kit["bb"][:, 0, :])
            dve.wait_ge(g_ps, 1)
            dve.tensor_scalar(g_sb[0:RG, :], psum[0:RG, 3, :], scl[0:RG, 0:1], None, ALU.mult).then_inc(g_ready, 1)
            for i in range(NT):
                dve.wait_ge(u_ps, i + 1)
                if i >= 2:
                    dve.wait_ge(h1t_ps, i - 1)
                    dve.wait_ge(u_hi, i - 1)
                dve.tensor_tensor(ua[:, i % 2, :], psum[:, 2 + 2 * (i % 2), :], kit["bb"][:, 0, :], ALU.add).then_inc(h1_ready, 1)
                dve.wait_ge(h1_ready, i + 1)
                dve.wait_ge(u_hi, i + 1)
                dve.scalar_tensor_tensor(hs[:, 0, 1, i, :], ua[:, i % 2, :], scl[:, 0:1], hs[:, 0, 0, i, :], ALU.mult, ALU.subtract).then_inc(u_lo, 1)
            dve.wait_ge(bb_in[1], 16)
            dve.wait_ge(h1t_ps, NT)
            for i in range(NT + 1):
                if i < NT:
                    dve.wait_ge(acc_ps, i + 1)
                    if i >= 2:
                        dve.wait_ge(m_ps, i - 1)
                    dve.scalar_tensor_tensor(ua[:, i % 2, :], psum[:, i % 2, :], scl[:, 1:2], kit["bb"][:, 1, :], ALU.mult, ALU.add).then_inc(acc_read, 1)
                if i:
                    j = i - 1
                    if j == 0:
                        dve.wait_ge(bb_in[0], 32)
                    dve.wait_ge(o_ps, j + 1)
                    y = kit["xin"][:, j % 2, :]
                    v = vt[:, :]
                    dve.tensor_tensor(v, psum[:, 4 + j % 2, :], kit["bb"][:, 0, :], ALU.add).then_inc(o_read, 1)
                    dve.wait_ge(o_read, j + 1)
                    dve.wait_ge(res_in[j % 2], 16 * (j // 2 + 1))
                    step(dve.scalar_tensor_tensor(v, v, 0.0, y, ALU.max, ALU.add))
                    st = lnst[:, j % 2, :]
                    step(dve.bn_stats(st[:, 0:6], v))
                    dve.bn_aggr(st[:, 6:8], st[:, 0:6]).then_inc(var_ready, 1)
                    norm_end(0, j, 0, st, v)

            def layernorm(n, i, k, y):
                st = lnst[:, i % 2, :]
                step(dve.bn_stats(st[:, 0:6], y))
                dve.bn_aggr(st[:, 6:8], st[:, 0:6]).then_inc(var_ready, 1)
                norm_end(n, i, k, st, y)

            if upto >= 3:
                kit = kits[1]
                for l in range(2):
                    r = 1 + l
                    scale(2, 520.0 if l == 0 else None)
                    for i in range(NT):
                        dve.wait_ge(gate_sig, tick(l, i))
                        dve.tensor_scalar(gates[:, i % 2, 2:4], gates[:, i % 2, 0:2], scl[:, 0:1], None, ALU.mult).then_inc(gate_ready, 1)
                        dve.wait_ge(gate_ready, tick(l, i))
                        dve.wait_ge(u_hi, tick(r, i))
                        for t in range(2):
                            x = dve.scalar_tensor_tensor(hs[:, t, 1, i, :], psum[:, 2 + 2 * (i % 2) + t, :], gates[:, i % 2, 2 + t:3 + t],
                                                         hs[:, t, 0, i, :], ALU.mult, ALU.subtract)
                        x.then_inc(u_lo, 1)
                    dve.wait_ge(bb_in[l], 16 * (3 if l == 0 else 2))
                    for i in range(NT):
                        dve.wait_ge(o_ps, tick(r, i))
                        dve.tensor_tensor(vt[:, :], psum[:, 4 + i % 2, :], kit["bb"][:, l, :], ALU.add).then_inc(o_read, 1)
                        dve.wait_ge(o_read, tick(r, i))
                        dve.wait_ge(acc_ps, tick(r, i))
                        if l == 0:
                            if i >= 2:
                                dve.wait_ge(t_ps, tick(r, i - 2))
                            dve.scalar_tensor_tensor(ua[:, i % 2, :], psum[:, i % 2, :], scl[:, 1:2], vt[:, :], ALU.mult, ALU.add).then_inc(acc_read, 1)
                            dve.wait_ge(acc_read, tick(r, i))
                        else:
                            dve.scalar_tensor_tensor(vt[:, :], psum[:, i % 2, :], scl[:, 1:2], vt[:, :], ALU.mult, ALU.add).then_inc(acc_read, 1)
                            dve.wait_ge(acc_read, tick(r, i))
                            t = NT + i
                            dve.wait_ge(res_in[i % 2], 16 * (t // 2 + 1))
                            step(dve.tensor_tensor(vt[:, :], vt[:, :], kit["xin"][:, i % 2, :], ALU.add))
                            layernorm(1, i, 1, vt[:, :])
                    if l == 0:
                        dve.wait_ge(v_ready, tick(0, NT - 1))
            if upto >= 4:
                kit = kits[2]
                for l in range(5):
                    r = 3 + l
                    scale(1, 520.0 if l == 0 else None)
                    for i in range(NT):
                        dve.wait_ge(u_hi, tick(r, i))
                        dve.scalar_tensor_tensor(hs[:, 0, 1, i, :], psum[:, 2 + i % 2, :], scl[:, 0:1],
                                                 hs[:, 0, 0, i, :], ALU.mult, ALU.subtract).then_inc(u_lo, 1)
                    dve.wait_ge(bb_in[r % 2], 16 * BB_COUNT[r])
                    step(dve.tensor_scalar(scl[:, 2:3], epsc[:, l:l + 1], 1.0, None, ALU.add))
                    for i in range(NT):
                        step(dve.tensor_tensor(vt[:, :], hs[:, 0, 0, i, :], hs[:, 0, 1, i, :], ALU.add))
                        dve.wait_ge(acc_ps, tick(r, i))
                        dve.scalar_tensor_tensor(vt[:, :], vt[:, :], scl[:, 2:3], psum[:, i % 2, :], ALU.mult, ALU.add).then_inc(acc_read, 1)
                        dve.wait_ge(acc_read, tick(r, i))
                        if i >= 2 and l < 4:
                            dve.wait_ge(t_ps, tick(r, i - 2))
                        dve.scalar_tensor_tensor(ua[:, i % 2, :], vt[:, :], scl[:, 1:2], kit["bb"][:, r % 2, :], ALU.mult, ALU.add).then_inc(v_pre, 1)
                        dve.wait_ge(v_pre, tick(V_OF[r] - 1, i))
                        if l == 4:
                            step(dve.tensor_scalar(ua[:, i % 2, :], ua[:, i % 2, :], 0.0, None, ALU.max))
                            dve.tensor_reduce(sml[:, i % 2, 0:1], ua[:, i % 2, :], AX.X, ALU.max, negate=True).then_inc(lsm_neg, 1)
                            dve.wait_ge(lsm_exp, i + 1)
                            step(dve.tensor_tensor(sml[:, i % 2, 3:4], sml[:, i % 2, 0:1], sml[:, i % 2, 2:3], ALU.subtract))
                            t = 2 * NT + i
                            dve.wait_ge(res_in[i % 2], 16 * (t // 2 + 1))
                            step(dve.scalar_tensor_tensor(vt[:, :], ua[:, i % 2, :], sml[:, i % 2, 3:4], kit["xin"][:, i % 2, :], ALU.add, ALU.add))
                            layernorm(2, i, 2, vt[:, :])
                    if l < 4:
                        dve.wait_ge(v_ready, tick(V_OF[r], NT - 1))
            if upto >= 5:
                dve.wait_ge(bb_in[0], 16 * BB_COUNT[8])
                for i in range(NT):
                    dve.wait_ge(acc_ps, tick(8, i))
                    dve.tensor_tensor(vt[:, :], psum[:, i % 2, :], kit["bb"][:, 0, :], ALU.add).then_inc(acc_read, 1)
                    dve.wait_ge(acc_read, tick(8, i))
                    t = 3 * NT + i
                    dve.wait_ge(res_in[i % 2], 16 * (t // 2 + 1))
                    step(dve.tensor_tensor(vt[:, :], vt[:, :], kit["xin"][:, i % 2, :], ALU.add))
                    layernorm(3, i, 2, vt[:, :])

        @block.scalar
        def _(act):
            act.wait_ge(ranges_ready, 1)
            with act.Fori(0, NW // GB) as g:
                for u in range(GB):
                    w = g * GB + u
                    b = u % 2
                    through = act.value_load(wrow_i[0:1, 2, bass.ds(w, 1)], min_val=1, max_val=NW * ER)
                    act.wait_ge(onehot_free[1], through + 1)
                    act.activation(adj[:, 0, :, bass.ds(w * W, W)], win[b][:, :, 0:W], ACT.Copy)
                    s = u // 8
                    if u % 8 == 0:
                        act.wait_ge(turn_ps, 12 * g + 6 * s + 6)
                    act.activation(typed[:, s, :, :, W * (u % 8):W * (u % 8) + W].rearrange("p m j d -> p j m d"),
                                   win[b][:, :, W:3 * W].rearrange("p j (m d) -> p j m d", m=2), ACT.Copy)
                    act.wait_ge(wparts_free[b], (GB // 2) * g + u // 2 + 1)
                    act.activation(wparts[:, b, :, :], win[b][:, :, 3 * W:6 * W], ACT.Copy).then_inc(win_free[b], 1)
                    if u in (10, 15):
                        s = u // 15
                        for q in range(6):
                            act.wait_ge(turn_ps, 6 * (2 * g + s) + q + 13)
                            if q < 3:
                                lot = typed_ps[q % 2]
                                if q == 1:
                                    for t in range(2):
                                        x = act.activation(adj[:, 1 + t, bass.ds(g * 2 + s, 1), (1 - t) * 1024:(1 - t) * 1024 + 512].rearrange("p o n -> p (o n)"),
                                                           lot[:, t * 512:t * 512 + 512], ACT.Copy)
                                else:
                                    x = act.activation(adj[:, 1 + q // 2, bass.ds(g * 2 + s, 1), q // 2 * 512:q // 2 * 512 + 1024].rearrange("p o n -> p (o n)"), lot, ACT.Copy)
                                x.then_inc(turned_out, 1)
                            else:
                                if q == 3:
                                    act.wait_ge(row_out, 16 * (2 * g + s + 1))
                                act.activation(aw_row[:, 512 * (q - 3):512 * (q - 2)], psum[:, 6 + q % 2, :], ACT.Copy).then_inc(turned_out, 1)

            act.drain().then_inc(built, 1)

            n_act = [0]

            def step(ins_):
                n_act[0] += 1
                ins_.then_inc(act_done, 1)
                act.wait_ge(act_done, n_act[0])

            act.wait_ge(built, 4)
            for i in range(NT):
                act.wait_ge(x_in[i % 2], 16 * (i // 2 + 1))
                if i >= 2:
                    act.wait_ge(x_sq, i - 1)
                act.activation(ua[:, i % 2, :], kits[0]["xin"][:, i % 2, :], ACT.Square, accum_out=norm2[:, i:i + 1]).then_inc(x_sq, 1)
                act.wait_ge(x_ps, i + 1)
                act.activation(xt[:, i, :, :].rearrange("p k n -> p (k n)"), psum[:, 6 + i % 2, :], ACT.Copy).then_inc(x_cp, 1)
            act.wait_ge(pb_ready, 1)
            act.wait_ge(proj_cp, 6)
            n = 0
            for a in range(9):
                for h in range(2):
                    for g in range(4):
                        n += 1
                        if n > 4:
                            act.wait_ge(tanh_used, n - 4)
                        r = 9 * g + a
                        act.activation(tanh[:, (n - 1) % 4, :], proj[:, h, :], ACT.Tanh, bias=pbias[:, h, r:r + 1]).then_inc(tanh_ready, 1)
            for i in range(NT):
                act.wait_ge(sm_neg, i + 1)
                q, k = i // 4, i % 4
                v = psum[:, 4 + q, P * k:P * k + P].rearrange("p (g c) -> p g c", g=4)[:, :, 0:9]
                act.activation(att[:, i % 2, :].rearrange("p (g c) -> p g c", g=4), v, ACT.Exp, bias=sml[:, i % 2, 0:1],
                               accum_out=sml[:, i % 2, 1:2]).then_inc(sm_exp, 1)

            seen = [0]

            def colnorms(slots):
                for b in slots:
                    for k in range(4):
                        seen[0] += 1
                        if seen[0] > 2:
                            act.wait_ge(sq_used, seen[0] - 2)
                        act.activation(ua[:, (seen[0] - 1) % 2, :], wb[:, b, k, :], ACT.Square).then_inc(sq_ready, 1)

            act.wait_ge(weights["wn"], 16)
            act.wait_ge(x_sq, NT)
            colnorms([0])
            act.wait_ge(scale_ready, 1)
            for i in range(NT):
                act.wait_ge(h1_ready, i + 1)
                act.activation(hs[:, 0, 0, i, :], ua[:, i % 2, :], ACT.Copy, scale=scl[:, 0:1]).then_inc(u_hi, 1)
                act.wait_ge(h1t_ps, i + 1)
                act.activation(xt[:, i, :, :].rearrange("p k n -> p (k n)"), psum[:, 6, :], ACT.Copy).then_inc(h1t_cp, 1)
            for i in range(NT + 1):
                if i < NT:
                    act.wait_ge(m_ps, i + 1)
                    if i >= 2:
                        act.wait_ge(o_ps, i - 1)
                    act.activation(kits[0]["mt"][:, i % 2, :, :].rearrange("p k n -> p (k n)"), psum[:, 6, :], ACT.Copy).then_inc(m_cp, 1)
                if i:
                    j = i - 1
                    act.wait_ge(var_ready, tick(0, j))
                    act.activation(lnst[:, j % 2, 8:9], lnst[:, j % 2, 7:8], ACT.Sqrt, bias=bcol[:, 5:6]).then_inc(std_ready, 1)
                    act.wait_ge(t_ps, tick(0, j))
                    act.activation(xt[:, j, :, :].rearrange("p k n -> p (k n)"), psum[:, 7, :], ACT.Copy).then_inc(t_cp, 1)
            if upto >= 2:
                for cc in range(64):
                    act.wait_ge(comb_ps, cc + 1)
                    o = cc // 8
                    if cc % 8 == 0 and o >= 2:
                        act.wait_ge(comb_out[o % 2], 64 * (o // 2))
                    act.activation(comb[:, o % 2, cc % 8, :], psum[:, cc % 2, :], ACT.Copy).then_inc(comb_cp, 1)

            def transposed(r, i):
                act.wait_ge(t_ps, tick(r, i))
                act.activation(xt[:, i, :, :].rearrange("p k n -> p (k n)"), psum[:, 7, :], ACT.Copy).then_inc(t_cp, 1)

            def std(n, i):
                act.wait_ge(var_ready, tick(n, i))
                act.activation(lnst[:, i % 2, 8:9], lnst[:, i % 2, 7:8], ACT.Sqrt, bias=bcol[:, 5:6]).then_inc(std_ready, 1)

            def relu(r, i):
                if r == 1:
                    act.wait_ge(acc_read, tick(r, i))
                else:
                    act.wait_ge(v_pre, tick(V_OF[r] - 1, i))
                step(act.activation(ua[:, i % 2, :], ua[:, i % 2, :], ACT.Relu))
                if r == 7:
                    return
                act.activation(kits[kit_of[r]]["mt"][:, i % 2, :, :].rearrange("p k n -> p (k n)"), ua[:, i % 2, :], ACT.Square,
                               accum_out=norm2[:, i:i + 1]).then_inc(v_ready, 1)

            if upto >= 3:
                for l in range(2):
                    r = 1 + l
                    act.wait_ge(weights["l1" + "ab"[l]], 48)
                    act.wait_ge(t_ps, tick(r - 1, NT - 1))
                    if l == 0:
                        act.wait_ge(comb_out[0], 256)
                        act.wait_ge(comb_out[1], 256)
                    colnorms([0, 1])
                    act.wait_ge(scale_ready, 2 + l)
                    for i in range(NT):
                        act.wait_ge(gate_ps, tick(l, i))
                        if i >= 2:
                            act.wait_ge(u_lo, tick(r, i - 2))
                        act.activation(gates[:, i % 2, 0:2], psum[:, 6 + i % 2, 0:2], ACT.Sigmoid).then_inc(gate_sig, 1)
                        act.wait_ge(gate_ready, tick(l, i))
                        act.wait_ge(u_ps, tick(r, i))
                        for t in range(2):
                            x = act.activation(hs[:, t, 0, i, :], psum[:, 2 + 2 * (i % 2) + t, :], ACT.Copy, scale=gates[:, i % 2, 2 + t:3 + t])
                        x.then_inc(u_hi, 1)
                    for i in range(NT + 1):
                        if l == 0:
                            if i < NT:
                                relu(r, i)
                        elif i < NT:
                            std(1, i)
                        if i:
                            transposed(r, i - 1)
            if upto >= 4:
                for l in range(5):
                    r = 3 + l
                    act.wait_ge(gin_in[l], 16)
                    act.wait_ge(t_ps, tick(r - 1, NT - 1))
                    colnorms([r % 2])
                    act.wait_ge(scale_ready, 4 + l)
                    for i in range(NT):
                        act.wait_ge(u_ps, tick(r, i))
                        act.activation(hs[:, 0, 0, i, :], psum[:, 2 + i % 2, :], ACT.Copy, scale=scl[:, 0:1]).then_inc(u_hi, 1)
                    for i in range(NT + 1):
                        if i < NT:
                            if l < 4:
                                relu(r, i)
                            else:
                                act.wait_ge(lsm_neg, i + 1)
                                step(act.activation(kits[2]["mt"][:, i % 2, :, :].rearrange("p k n -> p (k n)"), ua[:, i % 2, :], ACT.Exp,
                                                    bias=sml[:, i % 2, 0:1], accum_out=sml[:, i % 2, 1:2]))
                                act.activation(sml[:, i % 2, 2:3], sml[:, i % 2, 1:2], ACT.Ln).then_inc(lsm_exp, 1)
                                std(2, i)
                        if i:
                            transposed(r, i - 1)
            if upto >= 5:
                for i in range(NT):
                    act.wait_ge(u_ps, tick(8, i))
                    act.activation(sup[:, i, :], psum[:, 2 + i % 2, :], ACT.Copy).then_inc(u_hi, 1)
                for i in range(NT):
                    std(3, i)

        @block.tensor
        def _(pe):
            pe.wait_ge(c_ready, 8)
            pe.wait_ge(edges_in, 64)
            pe.wait_ge(erow_ready, 1)
            for a in range(4):
                for h in range(2):
                    c = 256 * (a % 2) + ER * h
                    x = pe.transpose(psum[:, a // 2, c:c + ER], erow[0:ER, a, P * h:P * h + P], ident[0:ER, 0:ER])
            x.then_inc(ecol_ps, 1)
            pe.wait_ge(span_ready, 4)
            for f in range(2):
                for h in range(2):
                    x = pe.transpose(psum[0:NW, 2 + f, ER * h:ER * h + ER], span[0:ER, f, h, :], ident[0:ER, 0:ER])
            x.then_inc(spant_ps, 1)
            pe.wait_ge(wcol_ready, 1)
            for f in range(2):
                x = pe.matmul(psum[0:1, 4, NW * f:NW * f + NW], wcol[0:NW, 2 + f:3 + f], ident[0:NW, 0:NW], start=True, stop=True)
            x.then_inc(wrow_ps, 1)
            pe.wait_ge(ranges_ready, 1)
            with pe.Fori(0, NW // GB) as g:
                for u in range(GB):
                    w = g * GB + u
                    b = u % 2
                    pairs = pe.value_load(wrow_i[0:1, 1, bass.ds(w, 1)], min_val=1, max_val=ER)
                    before = pe.value_load(wrow_i[0:1, 3, bass.ds(w, 1)], min_val=0, max_val=NW * ER)
                    pe.wait_ge(win_free[b], (GB // 2) * g + u // 2 + 1)
                    for j in range(0, NT, 4):
                        pe.matmul(win[b][:, j, 0:2], zeros, zeros[:, 0:2], start=True, stop=True, skip_group_check=True)
                    with pe.Fori(0, pairs) as q:
                        for k in range(2):
                            pe.wait_ge(onehot_ready[k], before + q + 1)
                            for j in range(NT):
                                x = pe.matmul(win[b][:, j, 0:NPART * W], onehot_s[:, k, P * j:P * j + P],
                                              onehot_d[:, k, :, :].rearrange("p v w -> p (v w)"), start=False, stop=True, skip_group_check=True)
                            x.then_inc(onehot_free[k], 1)
                    if u in (10, 15):
                        s = u // 15
                        for k in range(2):
                            pe.wait_ge(wparts_free[k], 8 * g + 4 * s + 5)
                        for q in range(6):
                            pe.wait_ge(turned_out, 6 * (2 * g + s) + q + 1)
                            if q < 3:
                                for n in range(8):
                                    t, j = divmod(8 * q + n, NT)
                                    x = pe.transpose(typed_ps[q % 2][:, P * n:P * n + P], typed[:, s, t, j, :], ident16[:])
                            else:
                                for n in range(4):
                                    x = pe.transpose(psum[:, 6 + q % 2, P * n:P * n + P], aw_stage[:, s, 4 * (q - 3) + n, :], ident[:])
                            x.then_inc(turn_ps, 1)
            pe.drain().then_inc(built, 1)

            pe.wait_ge(built, 4)
            for i in range(NT):
                pe.wait_ge(x_in[i % 2], 16 * (i // 2 + 1))
                if i >= 2:
                    pe.wait_ge(x_cp, i - 1)
                for k in range(4):
                    x = pe.transpose(psum[:, 6 + i % 2, P * k:P * k + P], kits[0]["xin"][:, i % 2, P * k:P * k + P], ident[:])
                x.then_inc(x_ps, 1)
            pe.wait_ge(weights["img"], 16)
            for k in range(8):
                x = pe.transpose(psum[:, 4, RG * k:RG * k + RG], img[0:RG, P * k:P * k + P], ident[0:RG, 0:RG])
            x.then_inc(imgt_ps, 1)
            pe.wait_ge(imgt_cp, 1)
            pe.wait_ge(weights["wi"], 16)
            for h in range(2):
                for k in range(8):
                    x = pe.matmul(psum[:, 5, RG * h:RG * h + RG], wi[:, k, P * h:P * h + P], img_t[:, k, :], start=k == 0, stop=k == 7)
            x.then_inc(ip_ps, 1)
            pe.wait_ge(x_cp, NT)
            pe.wait_ge(weights["wf"], 16)
            for q in range(6):
                h, c = q % 2, q // 2
                if q >= 2:
                    pe.wait_ge(proj_cp, q - 1)
                for k in range(4):
                    x = pe.matmul(psum[:, 6 + q % 2, :].rearrange("p (a n) -> p a n", a=4), wf[:, k, P * h:P * h + P], xt[:, 4 * c:4 * c + 4, k, :], start=k == 0, stop=k == 3)
                x.then_inc(proj_ps, 1)
            n = 0
            for a in range(9):
                for h in range(2):
                    for g in range(4):
                        n += 1
                        pe.wait_ge(tanh_ready, n)
                        for c in range(3):
                            x = pe.matmul(psum[32 * g:32 * g + 32, c, :], wa_pad[:, h, 31 - a:63 - a], tanh[:, (n - 1) % 4, 512 * c:512 * c + 512],
                                          start=a == 0 and h == 0, stop=a == 8 and h == 1)
                        x.then_inc(tanh_used, 1)
            pe.wait_ge(weights["wim"], 16)
            for k in range(8):
                x = pe.matmul(psum[0:RG, 3, :], img_t[:, k, :], wim[:, k, :], start=k == 0, stop=k == 7)
            x.then_inc(g_ps, 1)
            pe.wait_ge(lt_ready, 3)
            for q in range(3):
                for k in range(4):
                    i = 4 * q + k
                    x = pe.transpose(psum[:, 4 + q % 3, P * k:P * k + P], logit_t[:, P * i:P * i + P], ident[:])
                x.then_inc(ln_ps, 1)
            for i in range(NT):
                pe.wait_ge(att_ready, i + 1)
                if i >= 2:
                    pe.wait_ge(att_cp, i - 1)
                pe.transpose(psum[0:RG, i % 2, 0:P], att[:, i % 2, :], ident[:]).then_inc(att_ps, 1)

            seen = [0]

            def colnorms(slots, used):
                for b, _ in enumerate(slots):
                    for k in range(4):
                        seen[0] += 1
                        pe.wait_ge(sq_ready, seen[0])
                        x = pe.matmul(psum[:, b, :], ones[:], ua[:, (seen[0] - 1) % 2, :], start=k == 0, stop=k == 3)
                        x.then_inc(sq_used, 1)

            def rows(bank, i, w, first=True, last=True):
                for k in range(4):
                    x = pe.matmul(psum[:, bank, :], xt[:, i, k, :], w[:, k, :], start=first and k == 0, stop=last and k == 3)
                return x

            def aggregate(r, i, mats):
                n = 0
                for t, m in enumerate(mats):
                    for j in range(NT):
                        if i == 0 and t == 0:
                            pe.wait_ge(u_hi, tick(r, j))
                            pe.wait_ge(u_lo, tick(r, j))
                        for half in range(2):
                            n += 1
                            x = pe.matmul(psum[:, i % 2, :], adj[:, m, j, P * i:P * i + P], hs[:, t, half, j, :], start=n == 1,
                                          stop=n == 2 * NT * len(mats) and r > 0)
                return x

            def back(i):
                for k in range(4):
                    x = pe.transpose(psum[:, 7, P * k:P * k + P], src_t(i)[:, P * k:P * k + P], ident[:])
                return x

            pe.wait_ge(weights["wn"], 16)
            pe.wait_ge(att_cp, NT)
            colnorms([0], 0)
            pe.wait_ge(scale_ready, 1)
            for i in range(NT + 1):
                if i < NT:
                    if i >= 2:
                        pe.wait_ge(h1_ready, i - 1)
                    rows(2 + 2 * (i % 2), i, wb[:, 0, :, :]).then_inc(u_ps, 1)
                if i > 0:
                    pe.wait_ge(h1_ready, i)
                    if i > 1:
                        pe.wait_ge(h1t_cp, i - 1)
                    for k in range(4):
                        x = pe.transpose(psum[:, 6, P * k:P * k + P], ua[:, (i - 1) % 2, P * k:P * k + P], ident[:])
                    x.then_inc(h1t_ps, 1)
            pe.wait_ge(g_ready, 1)
            pe.wait_ge(weights["wt"], 16)
            pe.wait_ge(weights["wbm"], 16)
            pe.wait_ge(h1t_cp, NT)
            for i in range(NT + 2):
                if i < NT:
                    if i >= 2:
                        pe.wait_ge(acc_read, tick(0, i - 2))
                    aggregate(0, i, [0])
                    pe.matmul(psum[:, i % 2, :], att_t[0:RG, P * i:P * i + P], g_sb[0:RG, :], start=False, stop=True).then_inc(acc_ps, 1)
                if 0 < i <= NT:
                    j = i - 1
                    pe.wait_ge(acc_read, tick(0, j))
                    if j:
                        pe.wait_ge(m_cp, j)
                    for k in range(4):
                        x = pe.transpose(psum[:, 6, P * k:P * k + P], ua[:, j % 2, P * k:P * k + P], ident[:])
                    x.then_inc(m_ps, 1)
                    if j >= 2:
                        pe.wait_ge(o_read, tick(0, j - 2))
                    rows(4 + j % 2, j, wb[:, 0, :, :], last=False)
                    pe.wait_ge(m_cp, j + 1)
                    for k in range(4):
                        x = pe.matmul(psum[:, 4 + j % 2, :], kits[0]["mt"][:, j % 2, k, :], wb[:, 1, k, :], start=False, stop=k == 3)
                    x.then_inc(o_ps, 1)
                if i >= 2:
                    j = i - 2
                    pe.wait_ge(y_ready, tick(0, j))
                    if j:
                        pe.wait_ge(t_cp, tick(0, j - 1))
                    for k in range(4):
                        x = pe.transpose(psum[:, 7, P * k:P * k + P], kits[0]["yb"][:, j % 2, P * k:P * k + P], ident[:])
                    x.then_inc(t_ps, 1)
            if upto >= 2:
                pe.wait_ge(attw_ready, 2)
                pe.wait_ge(acc_read, tick(0, NT - 1))
                for cc in range(64):
                    pe.wait_ge(basis_in[cc % 4], 16 * (cc // 4 + 1))
                    if cc >= 2:
                        pe.wait_ge(comb_cp, cc - 1)
                    for g in range(4):
                        x = pe.matmul(psum[32 * g:32 * g + 32, cc % 2, :], attw[0:120, cc // 32, :], basis[0:120, cc % 4, D * g:D * g + D], start=True, stop=True)
                    x.then_inc(comb_ps, 1)

            def finish(r, i, src, ready):
                pe.wait_ge(ready, tick(V_OF[r] if ready is v_ready else NORM_OF[r], i))
                if i:
                    pe.wait_ge(t_cp, tick(r, i - 1))
                for k in range(4):
                    x = pe.transpose(psum[:, 7, P * k:P * k + P], src[:, i % 2, P * k:P * k + P], ident[:])
                x.then_inc(t_ps, 1)

            if upto >= 3:
                for l in range(2):
                    r = 1 + l
                    pe.wait_ge(t_cp, tick(r - 1, NT - 1))
                    pe.wait_ge(weights["l1" + "ab"[l]], 48)
                    pe.wait_ge(comb_cp, 64)
                    pe.wait_ge(acc_read, tick(r - 1, NT - 1))
                    colnorms([0, 1], 0)
                    for i in range(NT):
                        b = 2 + 2 * (i % 2)
                        if i >= 2:
                            pe.wait_ge(u_lo, tick(r, i - 2))
                            pe.wait_ge(gate_sig, tick(l, i - 2))
                        if i == 0:
                            pe.wait_ge(u_lo, tick(r - 1, NT - 1))
                            pe.wait_ge(acc_read, tick(r - 1, NT - 1))
                        for k in range(4):
                            x = pe.matmul(psum[:, 6 + i % 2, 0:2], xt[:, i, k, :], gw[:, l, k, :], start=k == 0, stop=k == 3)
                        x.then_inc(gate_ps, 1)
                        rows(b, i, wb[:, 0, :, :])
                        rows(b + 1, i, wb[:, 1, :, :]).then_inc(u_ps, 1)
                    src = ua if l == 0 else kits[1]["yb"]
                    for i in range(NT + 1):
                        if i < NT:
                            pe.wait_ge(acc_read, tick(r, i - 2))
                            aggregate(r, i, [1, 2]).then_inc(acc_ps, 1)
                            if i < 2:
                                pe.wait_ge(u_lo, tick(r, NT - 1))
                            pe.wait_ge(o_read, tick(r, i - 2))
                            rows(4 + i % 2, i, root).then_inc(o_ps, 1)
                        if i:
                            finish(r, i - 1, src, v_ready if l == 0 else y_ready)
            if upto >= 4:
                for l in range(5):
                    r = 3 + l
                    pe.wait_ge(t_cp, tick(r - 1, NT - 1))
                    pe.wait_ge(gin_in[l], 16)
                    pe.wait_ge(acc_read, tick(r - 1, NT - 1))
                    colnorms([r % 2], 0)
                    for i in range(NT):
                        pe.wait_ge(u_lo, tick(r, i - 2))
                        if i == 0:
                            pe.wait_ge(acc_read, tick(r - 1, NT - 1))
                        rows(2 + i % 2, i, wb[:, r % 2, :, :]).then_inc(u_ps, 1)
                    if l == 0:
                        pe.wait_ge(weights["as_in"], 16)
                    for i in range(NT + 1):
                        if i < NT:
                            pe.wait_ge(acc_read, tick(r, i - 2))
                            aggregate(r, i, [0]).then_inc(acc_ps, 1)
                        if i:
                            finish(r, i - 1, ua if l < 4 else kits[2]["yb"], v_ready if l < 4 else y_ready)
            if upto >= 5:
                r = 8
                pe.wait_ge(t_cp, tick(r - 1, NT - 1))
                pe.wait_ge(gin_in[5], 16)
                for i in range(NT):
                    pe.wait_ge(u_hi, tick(r, i - 2))
                    if i == 0:
                        pe.wait_ge(u_lo, tick(7, NT - 1))
                    rows(2 + i % 2, i, wb[:, 0, :, :]).then_inc(u_ps, 1)
                pe.wait_ge(weights["aw"], 16)
                for i in range(NT):
                    pe.wait_ge(acc_read, tick(r, i - 2))
                    for j in range(NT):
                        if i == 0:
                            pe.wait_ge(u_hi, tick(r, j))
                        x = pe.matmul(psum[:, i % 2, :], aw[:, j, P * i:P * i + P], sup[:, j, :], start=j == 0, stop=j == NT - 1)
                    x.then_inc(acc_ps, 1)


def kernel(**inputs):
    import numpy as np
    import concourse.bacc as bacc
    from concourse.bass_utils import run_bass_kernel_spmd

    nc = bacc.Bacc("TRN2", target_bir_lowering=False, num_devices=1)
    arrays, aps = {}, {}
    for name, a in inputs.items():
        a = np.ascontiguousarray(a)
        arrays[f"in_{name}"] = a
        aps[name] = nc.dram_tensor(f"in_{name}", a.shape, mybir.dt.from_np(a.dtype), kind="ExternalInput").ap()
    out = nc.dram_tensor("out", [N, D], F32, kind="ExternalOutput").ap()
    program(nc, aps, out)
    r = run_bass_kernel_spmd(nc, [arrays], core_ids=[0])
    return r.results[0]["out"]
```

```python
import concourse.bass as bass
from concourse import mybir
from contextlib import ExitStack

F32, F16, BF16 = mybir.dt.float32, mybir.dt.float16, mybir.dt.bfloat16
I32 = mybir.dt.int32
ALU, ACT, AX = mybir.AluOpType, mybir.ActivationFunctionType, mybir.AxisListType

P = 128
N, D = 1536, 512
NT = N // P
E = 26112
ET = E // P
EC = ET + 4
ER = ET // 2
W = 16
NW = N // W
STEP = 4
MOST = -(-ET // STEP)
NPART = 6
CHUNKS_OF = {1: 8, 2: 8, 3: 4, 4: 4, 5: 4, 6: 4, 7: 4, 8: 0}
V_OF = {1: 0, 3: 1, 4: 2, 5: 3, 6: 4, 7: 5}
NORM_OF = {0: 0, 2: 1, 7: 2, 8: 3}
R_OF = {n: r for r, n in NORM_OF.items()}
BB_COUNT = {3: 3, 4: 4, 5: 4, 6: 5, 7: 5, 8: 6}
MEASURED = (0, 2, 4, 5, 6, 7)
N_SMALL = 5 + 4
LO_BY = 4096.0
RG, PJ = 36, 256
FAR = 1000.0


def tick(r, i):
    return NT * r + i + 1


def program(nc, ins, out):
    with ExitStack() as ctx:
        def sb(name, shape, dt):
            return ctx.enter_context(nc.sbuf_tensor(name, shape, dt))

        def sem(name):
            return ctx.enter_context(nc.semaphore(name))

        adj = sb("adj", [P, 3, NT, N], F16)
        hs = sb("hs", [P, 2, 2, NT, D], F16)
        xt = sb("xt", [P, NT, 4, P], F32)
        ident = sb("ident", [P, P], F32)
        ident16 = sb("ident16", [P, P], F16)
        psum = ctx.enter_context(nc.psum_tensor("psum", [P, 8, 512], F32))
        hflat = hs[:, :, :, :, :].rearrange("p a b c d -> p (a b c d)")
        wb = sb("wb", [P, 2, 4, D], F32)
        ua = sb("ua", [P, 2, D], F32)
        vt = sb("vt", [P, D], F32)
        ones = sb("ones", [P, P], F32)
        img_t = sb("img_t", [P, 8, RG], F32)
        wa_pad = sb("wa_pad", [P, 2, 64], F32)
        pbias = sb("pbias", [P, 2, RG], F32)
        bcol = sb("bcol", [P, 8], F32)
        norm2 = sb("norm2", [P, NT], F32)
        sm = sb("sm", [P, 2, NT], F32)
        sml = sb("sml", [P, 2, 8], F32)
        lnst = sb("lnst", [P, 2, 12], F32)
        scl = sb("scl", [P, 8], F32)
        scl_i = sb("scl_i", [P, 2], I32)
        epsc = sb("epsc", [P, 8], F32)
        gates = sb("gates", [P, 2, 4], F32)
        gw = sb("gw", [P, 2, 4, 2], F32)
        attc = sb("attc", [P, 2, 2], F32)
        attm = sb("attm", [P, 4], F32)
        attw = sb("attw", [P, 2, 32], F32)

        def part(buf, byte, shape, dt=F32):
            n = 1
            for d in shape:
                n *= d
            v = buf[:, byte // 2:(byte + n * 4) // 2].bitcast(dt)
            if len(shape) == 1:
                return v
            names = "abcd"[:len(shape)]
            return v.rearrange(f"p ({' '.join(names)}) -> p {' '.join(names)}", **{k: n_ for k, n_ in zip(names, shape)})

        H1 = 2 * NT * D * 2
        wim = part(hflat, 0, [8, D])
        wi = part(hflat, 16384, [8, PJ])
        proj = part(hflat, H1, [2, N])
        x_first = part(hflat, H1, [9, D])
        att_t = part(hflat, H1 + 12288, [N])
        img = part(hflat, H1 + 18432, [1024])
        g2 = part(hflat, H1 + 18432, [D])
        g_t = part(hflat, H1 + 20480, [4, RG])
        att = part(hflat, H1 + 22528, [NT, RG])
        wf = wb[:, 0, :, 0:PJ]
        adj_flat = [adj[:, m, :, :].rearrange("p j n -> p (j n)") for m in range(3)]
        logit_t = part(adj_flat[2], 0, [N])
        LOGIT = (2, 3, 7)
        tanh = part(adj_flat[2], 0, [3, N])
        base = {0: (adj_flat[2], 18432), 1: (adj_flat[0], 8192), 2: (hflat, H1)}
        kit_of = [0, 1, 1, 2, 2, 2, 2, 2, 2]
        kits = {}
        for k, (buf, at0) in base.items():
            kits[k] = dict(xin=part(buf, at0, [2, D]), bb=part(buf, at0 + 4096, [2, D]),
                           mt=part(buf, at0 + 8192, [2, 4, P]), yb=part(buf, at0 + 12288, [2, D]))
        root = part(adj_flat[0], 0, [4, D])

        def squares_of(r):
            return ua if r - 1 in NORM_OF else kits[kit_of[r - 1]]["yb"]

        sup = part(hflat, 0, [NT, D])
        aw = part(adj[:, 1:3, :, :].rearrange("p m j n -> p (m j n)"), 0, [NT, N])
        xs_dram = [nc.dram_tensor(f"x{k}_scratch", [N, D], F32, kind="Internal").ap() for k in range(3)]
        as_dram = nc.dram_tensor("as_scratch", [P, NT * N], F16, kind="Internal").ap()
        ts_dram = nc.dram_tensor("ts_scratch", [P, NT * N], F16, kind="Internal").ap()
        wc_dram = [nc.dram_tensor(f"comb{k}_scratch", [8, P, D], F32, kind="Internal").ap() for k in range(2)]
        aw_dram = nc.dram_tensor("aw_scratch", [P, NT, N], F32, kind="Internal").ap()

        flat = hs[:, :, :, :, :].rearrange("p a b c d -> p (a b c d)")
        at = 0

        def lay(n, dt, shape_str=None, **kw):
            nonlocal at
            size = n * (2 if dt in (F16, BF16) else 4) // 2
            v = flat[:, at:at + size]
            at += size
            if dt != F16:
                v = v.bitcast(dt)
            return v.rearrange(shape_str, **kw) if shape_str else v

        erow_i = lay(4 * 256, I32, "p (a e) -> p a e", a=4)
        erow = lay(4 * 256, F32, "p (a e) -> p a e", a=4)
        ecol = lay(4 * EC, F32, "p (a t) -> p a t", a=4)
        wrem = lay(2 * EC, F32, "p (a t) -> p a t", a=2)
        vals = lay(EC * NPART, BF16, "p (t v) -> p t v", v=NPART)
        iota_s = lay(N, F16)
        onehot_s = lay(STEP * N, F16, "p (k s) -> p k s", k=STEP)
        onehot_d = lay(STEP * NPART * W, BF16, "p (k v w) -> p k v w", k=STEP, v=NPART)
        basis = [flat[:, 0:4 * D * 2].bitcast(F32), lay(4 * D, F32)]
        aw_stage = xt[:, :, :, :].rearrange("p a b d -> p (a b d)")[:, 0:2 * NT * P].rearrange("p (k j d) -> p k j d", k=2, j=NT)
        span = lay(2 * 2 * NW, F32, "p (f h w) -> p f h w", f=2, h=2)
        spant = lay(2 * NW, F32, "p (h w) -> p h w", h=2)
        trange = lay(4, F32)
        win16 = lay(NW, F32)
        tileno = lay(4, F32)
        wcol = lay(8, F32)
        wrow = lay(4 * NW, F32, "p (a w) -> p a w", a=4)
        wrow_i = lay(4 * NW, I32, "p (a w) -> p a w", a=4)
        zeros = lay(P, BF16)
        rest = xt[:, :, :, :].rearrange("p a b d -> p (a b d)")[:, 2 * NT * P:]
        wparts = rest[:, 0:2 * NT * 3 * W].rearrange("p (k j c) -> p k j c", k=2, j=NT)
        wsum = rest[:, 2 * NT * 3 * W:2 * NT * 4 * W].rearrange("p (k j c) -> p k j c", k=2, j=NT)
        aw_row = rest[:, 2 * NT * 4 * W:2 * NT * 4 * W + N]
        typed = wb[:, :, :, :].rearrange("p a b n -> p (a b n)").bitcast(F16)[:, 0:2 * 2 * NT * P].rearrange("p (k m j d) -> p k m j d", k=2, m=2, j=NT)
        assert at <= 2 * 2 * NT * D

        c_ready = sem("c_ready")
        edges_in = sem("edges_in")
        side_ps, side_out = sem("side_ps"), sem("side_out")
        erow_ready = sem("erow_ready")
        ecol_ps = sem("ecol_ps")
        span_ready = sem("span_ready")
        spant_ps = sem("spant_ps")
        wcol_ready = sem("wcol_ready")
        wrow_ps = sem("wrow_ps")
        ranges_ready = sem("ranges_ready")
        onehot_ready = [sem(f"onehot_ready{k}") for k in range(STEP)]
        onehot_free = [sem(f"onehot_free{k}") for k in range(STEP)]
        win_free = [sem(f"win_free{b}") for b in range(2)]
        wparts_free = [sem(f"wparts_free{b}") for b in range(2)]
        wsum_ready = [sem(f"wsum_ready{b}") for b in range(2)]
        row_out = sem("row_out")
        dve_done = sem("dve_done")

        built = sem("built")
        weights = {k: sem("in_" + k) for k in ("wf", "wi", "img", "wim", "small", "wn", "wt", "wbm", "ts_out", "ts_in", "root", "l1a", "l1b", "aw", "att", "as_out", "as_in")}
        gin_in = [sem(f"gin_in{k}") for k in range(6)]
        x_in = [sem(f"x_in{k}") for k in range(NT // 3)]
        x_ps, x_cp, x_sq = sem("x_ps"), sem("x_cp"), sem("x_sq")
        proj_ps, proj_cp = sem("proj_ps"), sem("proj_cp")
        imgt_ps, imgt_cp, ip_ps, pb_ready = sem("imgt_ps"), sem("imgt_cp"), sem("ip_ps"), sem("pbias_ready")
        tanh_ready, tanh_used = sem("tanh_ready"), sem("tanh_used")
        lt_ready, ln_ps, logit_ready, exp_ready, att_ready, att_ps, att_cp = [sem(x) for x in (
            "logit_t_ready", "logit_ps", "logit_ready", "exp_ready", "att_ready", "att_ps", "att_t_ready")]
        gt_ps, gt_ready, g2_ps, g2_ready = sem("gt_ps"), sem("gt_ready"), sem("g2_ps"), sem("g2_ready")
        seen_ps, seen_read = sem("attended_ps"), sem("attended_read")
        sq_ready, sq_used, col_read = sem("sq_ready"), sem("sq_used"), sem("colnorms_read")
        r2_col, r2_all, scale_ready = sem("rownorm_col"), sem("rownorm_all"), sem("scale_ready")
        u_ps, u_hi, u_lo = sem("u_ps"), sem("u_hi"), sem("u_lo")
        h1_ready, h1t_ps, h1t_cp = sem("h1_ready"), sem("h1t_ps"), sem("h1t_cp")
        acc_ps, acc_read = sem("acc_ps"), sem("acc_read")
        m_ps, m_cp = sem("m_ps"), sem("m_cp")
        o_ps, o_read = sem("o_ps"), sem("o_read")
        relu_ready = sem("relu_ready")
        v_pre, v_ready = sem("v_pre"), sem("v_ready")
        t_ps, t_cp = sem("t_ps"), sem("t_cp")
        var_ready, std_ready = sem("var_ready"), sem("std_ready")
        y_ready, y_out = sem("y_ready"), [sem(f"y_out{k}") for k in range(2)]
        res_in = [sem(f"res_in{k}") for k in range(2)]
        gate_ps, gate_sig, gate_ready = sem("gate_ps"), sem("gate_sig"), sem("gate_ready")
        norm_ready = sem("norm_ready")
        lsm_neg, lsm_exp = sem("lsm_negmax"), sem("lsm_lnsum")
        basis_in = [sem(f"basis_in{k}") for k in range(2)]
        comb_out = [sem(f"comb_out{k}") for k in range(2)]
        act_done = sem("act_done")
        attw_ready = sem("attw_ready")
        bb_in = [sem(f"bb_in{k}") for k in range(2)]
        fin = sem("fin")

        block = ctx.enter_context(nc.Block())
        GB = 24
        NB = NW // GB
        HB = GB // 2
        BLOCKS = GB * W // P
        CH = 2 * 32 // NB
        side, by_window = [], {u: [] for u in range(GB)}
        for u in range(GB):
            here = []
            for s in range(BLOCKS):
                if u == GB - 1 and s == BLOCKS - 1:
                    here += [("turn", s, q) for q in range(6)]
                elif s < BLOCKS - 1 and 8 * (s + 1) < u <= 8 * (s + 1) + 3:
                    here += [("turn", s, 2 * (u - 8 * (s + 1) - 1) + q) for q in range(2)]
            if u % 3 != 2:
                n = 2 * (u // 3) + u % 3
                here.append(("basis", n // (CH // 2), n % (CH // 2)))
            for what in here:
                by_window[u].append((len(side),) + what)
                side.append(what)
        NS = len(side)
        assert NS % 2 == 0
        lot_of = {what: n for n, what in enumerate(side)}

        def side_at(g, n):
            return NS * g + n + 1 + NS

        def stage_free_at(g, s):
            last = lot_of[("turn", s - 2 if s >= 2 else (BLOCKS - 1 if s == 0 else 1), 5)]
            return side_at(g, last) - (0 if s >= 2 else NS)

        def side_copied(g, n):
            return NS * g + n + 3

        win = [psum[:, 3 * b:3 * b + 3, :].rearrange("p k c -> p (k c)").rearrange("p (j c) -> p j c", j=NT)
               for b in range(2)]

        bases = [ins[f"L1_gnn_basis{l + 1}"].rearrange("b (j i) o -> (b j) (i o)", j=4) for l in range(2)]
        combs = [wc_dram[l].rearrange("j (c q) o -> q j c o", q=4) for l in range(2)]

        FIRST_BITS, STEPS_BITS = ET.bit_length(), MOST.bit_length()
        PACKED = ((NW * MOST) << (FIRST_BITS + STEPS_BITS)) + (ET << STEPS_BITS) + MOST

        def unpack(v):
            why = "packed from values within these bounds"
            return (nc.s_assert_within((v >> STEPS_BITS) & ((1 << FIRST_BITS) - 1), 0, ET - 1, skip_runtime_bounds_check_because=why),
                    nc.s_assert_within(v & ((1 << STEPS_BITS) - 1), 1, MOST, skip_runtime_bounds_check_because=why),
                    nc.s_assert_within(v >> (FIRST_BITS + STEPS_BITS), 0, NW * MOST, skip_runtime_bounds_check_because=why))

        @block.sync
        def _(sp):
            for a, name in enumerate(("src", "dst", "edge_type_2")):
                sp.dma_start(erow_i[0:ER, a, :], ins[name].rearrange("(r e) -> r e", e=256)).then_inc(edges_in, 16)
            sp.dma_start(erow[0:ER, 3, :], ins["edge_weight"].rearrange("(r e) -> r e", e=256)).then_inc(edges_in, 16)
            for l in range(2):
                for t in range(2):
                    for j in range(4):
                        sp.dma_start(attc[j:120:4, l, t:t + 1], ins[f"L1_gnn_att{l + 1}"][t].unsqueeze(1),
                                     allow_slow_non_contiguous=True).then_inc(weights["att"], 16)

            def load_chunk(g, n):
                l, c = n // (CH // 2), g * (CH // 2) + n % (CH // 2)
                sp.dma_start(basis[n % 2][0:120, :], bases[l][:, bass.ds(c * (4 * D), 4 * D)]).then_inc(basis_in[n % 2], 16)

            def chunks(g, following):
                for n in range(CH):
                    l, c = n // (CH // 2), g * (CH // 2) + n % (CH // 2)
                    lot = lot_of[("basis", l, n % (CH // 2))]
                    if n < CH - 2 or following:
                        sp.wait_ge(side_ps, side_at(g, lot))
                        load_chunk(*((g, n + 2) if n < CH - 2 else (g + 1, n + 2 - CH)))
                    sp.wait_ge(side_out, side_copied(g, lot))
                    for q in range(4):
                        sp.dma_start(combs[l][q, :, bass.ds(c, 1), :].rearrange("j c o -> j (c o)"), ua[32 * q:32 * q + 8, n % 2, :]).then_inc(comb_out[n % 2], 16)

            sp.wait_ge(ecol_ps, 1)
            sp.wait_ge(span_ready, 4)
            load_chunk(0, 0)
            load_chunk(0, 1)
            with sp.Fori(0, NB - 1) as g:
                chunks(g, True)
            chunks(NB - 1, False)
            sp.wait_ge(row_out, 16 * (NT + 1))

            sp.wait_ge(built, 4)

            def x_tile(src, i):
                return src[P * i:P * i + P, :]

            x3 = ins["x"].rearrange("(g k p) d -> g p k d", p=P, k=3)
            for g in range(NT // 3):
                if g == 3:
                    sp.dma_start(wf, ins["L0_gnn_Wf"].rearrange("(k p) n -> p k n", p=P)).then_inc(weights["wf"], 16)
                    sp.wait_ge(x_ps, 3 * (g - 2))
                    sp.wait_ge(x_sq, 3 * (g - 2))
                sp.dma_start(x_first[:, 3 * (g % 3):3 * (g % 3) + 3, :], x3[g]).then_inc(x_in[g], 16)
            small = [
                (bcol[:, 0:2], ins["L0_gnn_bf"].rearrange("(k p) -> p k", p=P)),
                (bcol[:, 2:4], ins["L0_gnn_bi"].rearrange("(k p) -> p k", p=P)),
                (bcol[:, 4:5], ins["L0_gnn_ba"].unsqueeze(0).broadcast_to([P, 1])),
                (wa_pad[:, :, 31:32], ins["L0_gnn_Wa"].rearrange("(k p) o -> p k o", p=P)),
                (epsc[:, 0:5], ins["L2_gnn_eps"].unsqueeze(0).broadcast_to([P, 5])),
            ]
            for l in range(2):
                for t in range(2):
                    small.append((gw[:, l, :, t], ins[f"L1_gnn_gate_w{l + 1}"][t].rearrange("(k p) o -> p (k o)", p=P)))
            for to, of in small:
                sp.dma_start(to, of, allow_slow_non_contiguous=True).then_inc(weights["small"], 16)
            assert len(small) == N_SMALL

            sp.dma_start(ts_dram, adj_flat[2]).then_inc(weights["ts_out"], 16)
            sp.dma_start(as_dram, adj_flat[0]).then_inc(weights["as_out"], 16)

            def bias(slot, k, of):
                sp.dma_start(kits[k]["bb"][:, slot, :], of.unsqueeze(0).broadcast_to([P, D])).then_inc(bb_in[slot], 16)

            sp.wait_ge(weights["ts_out"], 16)
            bias(0, 0, ins["L0_gnn_bn"])
            bias(1, 0, ins["L0_gnn_bim"])
            wap = ins["L0_gnn_Wap"].rearrange("(h k p) n -> h p k n", h=2, p=P)
            sp.wait_ge(proj_ps, 6)
            sp.dma_start(wb[:, 0, :, :], wap[0]).then_inc(weights["wt"], 16)
            sp.wait_ge(u_ps, tick(0, NT - 1))
            sp.dma_start(wb[:, 1, :, :], wap[1]).then_inc(weights["wbm"], 16)
            sp.wait_ge(h1_ready, NT)
            bias(0, 0, ins["L0_gnn_bap"])

            def norm_tiles(n, k, src, dst, early=None):
                for i in range(NT + 2):
                    if i == 2 and early:
                        early()
                    if i < NT:
                        if i >= 2:
                            sp.wait_ge(var_ready, tick(n, i - 2))
                        sp.dma_start(kits[k]["xin"][:, i % 2, :], x_tile(src, i)).then_inc(res_in[i % 2], 16)
                    if i >= 2:
                        sp.wait_ge(y_ready, tick(n, i - 2))
                        sp.dma_start(x_tile(dst, i - 2), kits[k]["yb"][:, i % 2, :]).then_inc(y_out[i % 2], 16)

            def relations(l):
                for t in range(2):
                    sp.dma_start(wb[:, t, :, :], wc_dram[l][4 * t:4 * t + 4].rearrange("j p o -> p j o")).then_inc(weights["l1" + "ab"[l]], 16)

            def roots(l):
                sp.dma_start(root, ins[f"L1_gnn_root{l + 1}"].rearrange("(k p) n -> p k n", p=P)).then_inc(weights["root"], 16)

            def first_of_l1():
                for k in range(2):
                    sp.wait_ge(comb_out[k], 64 * 33)
                sp.wait_ge(o_ps, tick(0, NT - 1))
                sp.wait_ge(acc_ps, tick(0, NT - 1))
                sp.wait_ge(g2_ps, 1)
                sp.wait_ge(weights["as_out"], 16)
                relations(0)
                roots(0)
                sp.wait_ge(o_read, tick(0, NT - 1))
                for l in range(2):
                    bias(l, 1, ins[f"L1_gnn_bias{l + 1}"])

            def gin_weights(l):
                r = 3 + l
                w_in = ins["L2_gnn_W1"] if l == 0 else ins["L2_gnn_Ws"][l - 1]
                sp.dma_start(wb[:, r % 2, :, :], w_in.rearrange("(k p) n -> p k n", p=P)).then_inc(gin_in[l], 16)

            def gin_bias(l):
                bias((3 + l) % 2, 2, ins["L2_gnn_b1"] if l == 0 else ins["L2_gnn_bs"][l - 1])

            norm_tiles(0, 0, ins["x"], xs_dram[0], early=first_of_l1)
            for k in range(2):
                sp.wait_ge(y_out[k], 16 * 6)
            sp.wait_ge(t_ps, tick(0, NT - 1))
            sp.dma_start(adj_flat[2], ts_dram).then_inc(weights["ts_in"], 16)
            sp.wait_ge(u_ps, tick(1, NT - 1))
            relations(1)
            sp.wait_ge(o_ps, tick(1, NT - 1))
            roots(1)
            sp.wait_ge(u_ps, tick(2, NT - 1))
            gin_weights(0)
            norm_tiles(1, 1, xs_dram[0], xs_dram[1])
            gin_weights(1)
            sp.wait_ge(acc_ps, tick(2, NT - 1))
            gin_bias(0)
            gin_bias(1)
            for k in range(2):
                sp.wait_ge(y_out[k], 16 * 12)
            sp.wait_ge(t_ps, tick(2, NT - 1))
            sp.dma_start(adj_flat[0], as_dram).then_inc(weights["as_in"], 16)
            sp.dma_start(aw, aw_dram).then_inc(weights["aw"], 16)
            for l in range(2, 5):
                sp.wait_ge(u_ps, tick(1 + l, NT - 1))
                gin_weights(l)
                sp.wait_ge(v_pre, tick(V_OF[1 + l] - 1, NT - 1))
                gin_bias(l)
            sp.wait_ge(u_ps, tick(6, NT - 1))
            sp.dma_start(wb[:, 0, :, :], ins["L3_gnn_weight"].rearrange("(k p) n -> p k n", p=P)).then_inc(gin_in[5], 16)
            sp.wait_ge(v_pre, tick(V_OF[6] - 1, NT - 1))
            bias(0, 2, ins["L3_gnn_bias"])
            norm_tiles(2, 2, xs_dram[1], xs_dram[2])
            norm_tiles(3, 2, xs_dram[2], out)
            for k in range(2):
                sp.wait_ge(y_out[k], 16 * 6 * 4)

        @block.gpsimd
        def _(pool):
            pool.memset(ident[:], 0.0).then_inc(c_ready, 1)
            pool.wait_ge(c_ready, 1)
            pool.affine_select(out=ident[:], in_=ident[:], compare_op=ALU.not_equal, fill=1.0, base=0,
                               pattern=[[-1, P]], channel_multiplier=1).then_inc(c_ready, 1)
            pool.wait_ge(c_ready, 2)
            pool.tensor_copy(ident16[:], ident[:])
            pool.memset(zeros, 0.0)
            pool.memset(ones[:], 1.0)
            pool.memset(wa_pad[:], 0.0)
            pool.memset(attw[:], 0.0)
            pool.memset(bcol[:, 5:6], 1e-5).then_inc(c_ready, 1)
            pool.iota(iota_s, [[1, N]], base=0, channel_multiplier=0,
                      allow_small_or_imprecise_dtypes=True).then_inc(c_ready, 1)
            pool.iota(win16, [[W, NW]], base=0, channel_multiplier=0,
                      allow_small_or_imprecise_dtypes=True).then_inc(c_ready, 1)
            pool.iota(tileno[:, 0:2], [[1, 2]], base=1, channel_multiplier=2,
                      allow_small_or_imprecise_dtypes=True).then_inc(c_ready, 1)
            pool.iota(tileno[:, 2:4], [[-1, 2]], base=int(FAR), channel_multiplier=-2,
                      allow_small_or_imprecise_dtypes=True).then_inc(c_ready, 1)
            for k in range(STEP):
                pool.sem_inc(onehot_free[k], 1)
            for k in range(2):
                pool.sem_inc(comb_out[k], 64)
                pool.sem_inc(win_free[k], 1)
                pool.sem_inc(wparts_free[k], 1)
            pool.sem_inc(row_out, 16)
            pool.sem_inc(side_out, 2)
            pool.sem_inc(side_ps, NS)
            with pool.Fori(0, NB) as g:
                for u in range(GB):
                    b, s = u % 2, u // 8
                    if u % 8 == 0:
                        pool.wait_ge(side_ps, stage_free_at(g, s))
                    pool.wait_ge(win_free[b], HB * g + u // 2 + 2)
                    part = [wparts[:, b, :, W * v:W * v + W] for v in range(3)]
                    pool.tensor_tensor(wsum[:, b, :, :], part[0], part[1], ALU.add).then_inc(wsum_ready[b], 1)
                    pool.wait_ge(wsum_ready[b], HB * g + u // 2 + 1)
                    pool.tensor_tensor(aw_stage[:, s % 2, :, W * (u % 8):W * (u % 8) + W],
                                       wsum[:, b, :, :], part[2], ALU.add).then_inc(wparts_free[b], 1)

            pool.drain().then_inc(built, 1)

            n_all = 0
            for r in [0, 2, 3, 4, 5, 6, 7, 8]:
                if r in MEASURED:
                    n_all += 1
                    pool.wait_ge(r2_col, n_all)
                    pool.partition_all_reduce(scl[:, 5:6], scl[:, 4:5], P, bass.bass_isa.ReduceOp.max).then_inc(r2_all, 1)

        @block.vector
        def _(dve):
            n_dve = [0]

            def step(ins_):
                n_dve[0] += 1
                ins_.then_inc(dve_done, 1)
                dve.wait_ge(dve_done, n_dve[0])

            dve.wait_ge(c_ready, 7)
            dve.wait_ge(edges_in, 64)
            dve.tensor_copy(erow[0:ER, 0:3, :], erow_i[0:ER, 0:3, :]).then_inc(erow_ready, 1)
            dve.wait_ge(erow_ready, 1)
            dst2 = erow[0:ER, 1, :].rearrange("p (h e) -> p h e", h=2)
            dve.tensor_reduce(trange[0:ER, 0:2], dst2, AX.X, ALU.min)
            step(dve.tensor_reduce(trange[0:ER, 2:4], dst2, AX.X, ALU.max))
            step(dve.tensor_scalar(trange[0:ER, 0:2], trange[0:ER, 0:2], float(-W), None, ALU.add))
            for h in range(2):
                dve.tensor_scalar(spant[0:ER, h, :], win16[0:ER, :], trange[0:ER, h:h + 1], None, ALU.is_gt)
            step(dve.tensor_copy(wcol[0:ER, 0:1], tileno[0:ER, 0:1]))
            for h in range(2):
                x = dve.scalar_tensor_tensor(spant[0:ER, h, :], win16[0:ER, :], trange[0:ER, 2 + h:3 + h],
                                         spant[0:ER, h, :], ALU.is_le, ALU.mult)
            step(x)
            for f in range(2):
                for h in range(2):
                    k = 2 * (1 - f) + h
                    x = dve.tensor_scalar(span[0:ER, f, h, :], spant[0:ER, h, :], tileno[0:ER, k:k + 1], None, ALU.mult)
                    x.then_inc(span_ready, 1)
            dve.memset(ecol[:, :, ET:EC], -1.0)
            dve.wait_ge(ecol_ps, 1)
            for a in range(4):
                v = psum[:, a // 2, 256 * (a % 2):256 * (a % 2) + 2 * ER].rearrange("p (h r) -> p h r", h=2)
                x = dve.tensor_copy(ecol[:, a, 0:ET].rearrange("p (r h) -> p h r", h=2), v)
            step(x)
            dve.memset(vals[:, :, 0:1], 1.0)
            dve.tensor_scalar(vals[:, 0:EC, 1], ecol[:, 2, :], 0.0, None, ALU.is_equal)
            dve.tensor_scalar(vals[:, 0:EC, 2], ecol[:, 2, :], 0.0, None, ALU.not_equal)
            step(dve.tensor_copy(vals[:, 0:EC, 3], ecol[:, 3, :]))
            step(dve.tensor_tensor(wrem[:, 0, :], ecol[:, 3, :], vals[:, 0:EC, 3], ALU.subtract))
            step(dve.tensor_copy(vals[:, 0:EC, 4], wrem[:, 0, :]))
            step(dve.tensor_tensor(vals[:, 0:EC, 5], wrem[:, 0, :], vals[:, 0:EC, 4], ALU.subtract))
            dve.wait_ge(spant_ps, 1)
            for f in range(2):
                v = psum[0:NW, 2 + f, 0:2 * ER]
                x = dve.tensor_reduce(wcol[0:NW, f:f + 1], v, AX.X, ALU.max)
            step(x)
            step(dve.tensor_scalar(wcol[0:NW, 2:3], wcol[0:NW, 0:1], -1.0, FAR, ALU.mult, ALU.add))
            step(dve.tensor_scalar(wcol[0:NW, 2:3], wcol[0:NW, 2:3], float(ET - 1), None, ALU.min))
            step(dve.tensor_tensor(wcol[0:NW, 3:4], wcol[0:NW, 1:2], wcol[0:NW, 2:3], ALU.subtract))
            step(dve.tensor_scalar(wcol[0:NW, 3:4], wcol[0:NW, 3:4], 1.0, None, ALU.max))
            dve.tensor_scalar(wcol[0:NW, 3:4], wcol[0:NW, 3:4], 1.0 / STEP, 0.5 - 0.5 / STEP, ALU.mult, ALU.add).then_inc(wcol_ready, 1)
            dve.wait_ge(wrow_ps, 1)
            v = psum[0:1, 4, 0:2 * NW].rearrange("p (a w) -> p a w", a=2)
            step(dve.tensor_copy(wrow_i[0:1, 0:2, :], v))
            step(dve.tensor_copy(wrow[0:1, 0:2, :], wrow_i[0:1, 0:2, :]))
            step(dve.tensor_tensor_scan(wrow[0:1, 2, :], wrow[0:1, 1, :], wrow[0:1, 1, :], 0.0, ALU.add, ALU.bypass))
            step(dve.tensor_tensor(wrow[0:1, 3, :], wrow[0:1, 2, :], wrow[0:1, 1, :], ALU.subtract))
            step(dve.tensor_copy(wrow_i[0:1, 2:4, :], wrow[0:1, 2:4, :]))
            step(dve.tensor_scalar(wrow_i[0:1, 3, :], wrow_i[0:1, 3, :], FIRST_BITS + STEPS_BITS, None, ALU.logical_shift_left))
            step(dve.tensor_scalar(wrow_i[0:1, 0, :], wrow_i[0:1, 0, :], STEPS_BITS, None, ALU.logical_shift_left))
            step(dve.tensor_tensor(wrow_i[0:1, 0, :], wrow_i[0:1, 0, :], wrow_i[0:1, 1, :], ALU.bitwise_or))
            dve.tensor_tensor(wrow_i[0:1, 0, :], wrow_i[0:1, 0, :], wrow_i[0:1, 3, :], ALU.bitwise_or).then_inc(ranges_ready, 1)
            dve.wait_ge(ranges_ready, 1)

            dve.wait_ge(weights["att"], 16 * 16)
            step(dve.tensor_reduce(attm[0:120, :], ident[0:120, 0:120].rearrange("p (b j) -> p j b", j=4), AX.X, ALU.add))
            for l in range(2):
                for t in range(2):
                    x = dve.tensor_scalar(attw[0:120, l, 4 * t:4 * t + 4], attm[0:120, :], attc[0:120, l, t:t + 1], None, ALU.mult)
                x.then_inc(attw_ready, 1)

            def window(w):
                return dve.value_load(wrow_i[0:1, 0, bass.ds(w, 1)], min_val=0, max_val=PACKED)

            with dve.Fori(0, NB) as g:
                following = window(g * GB)
                for u in range(GB):
                    w = g * GB + u
                    first, steps, before = unpack(following)
                    if u + 1 < GB:
                        following = window(w + 1)
                    with dve.Fori(0, steps) as q:
                        for k in range(STEP):
                            t = nc.s_assert_within(first + STEP * q + k, 0, EC - 1, skip_runtime_bounds_check_because="a window's steps end less than a step past its last tile")
                            dve.wait_ge(onehot_free[k], before + q + 1)
                            dve.tensor_scalar(onehot_s[:, k, :], iota_s, ecol[:, 0, bass.ds(t, 1)], None, ALU.is_equal)
                            dve.scalar_tensor_tensor(
                                onehot_d[:, k, :, :], iota_s[:, bass.ds(w * W, W)].unsqueeze(1).broadcast_to([P, NPART, W]),
                                ecol[:, 1, bass.ds(t, 1)], vals[:, bass.ds(t, 1), :].rearrange("p o v -> p (o v)").unsqueeze(2).broadcast_to([P, NPART, W]),
                                ALU.is_equal, ALU.mult).then_inc(onehot_ready[k], 1)
            dve.drain().then_inc(built, 1)

            dve.wait_ge(built, 4)
            def x_turned(tiles):
                for i in tiles:
                    dve.wait_ge(x_ps, i + 1)
                    dve.tensor_copy(xt[:, i, :, :].rearrange("p k n -> p (k n)"), psum[:, 6 + i % 2, :]).then_inc(x_cp, 1)

            x_turned(range(9))
            dve.wait_ge(weights["small"], 16 * N_SMALL)
            dve.wait_ge(imgt_ps, 1)
            dve.tensor_copy(img_t[:, :, :].rearrange("p k r -> p (k r)"), psum[:, 4, 0:8 * RG]).then_inc(imgt_cp, 1)
            dve.wait_ge(ip_ps, 1)
            for h in range(2):
                x = dve.tensor_scalar(pbias[:, h, :], psum[:, 5, RG * h:RG * h + RG], bcol[:, 2 + h:3 + h], bcol[:, h:h + 1], ALU.add, ALU.add)
            x.then_inc(pb_ready, 1)
            x_turned(range(9, NT))
            dve.wait_ge(x_sq, NT)
            for q in range(6):
                h, c = q % 2, q // 2
                dve.wait_ge(proj_ps, q + 1)
                dve.tensor_copy(proj[:, h, 512 * c:512 * c + 512], psum[:, 6 + q % 2, :]).then_inc(proj_cp, 1)
            seen = [0]

            def column_max(bank, n_slots):
                seen[0] += 4 * n_slots
                dve.wait_ge(sq_used, seen[0])
                dve.tensor_reduce(scl[:, 3:4], psum[:, bank:bank + n_slots, :].rearrange("p b c -> p (b c)"), AX.X, ALU.max).then_inc(col_read, 1)

            def next_column_max(i, r):
                if i == 10 and r < 8:
                    column_max(2, 2 if r in (1, 2) else 1)

            def scale(bound2=None, bias_ap=None):
                if bound2 is None:
                    dve.tensor_reduce(scl[:, 4:5], norm2[:], AX.X, ALU.max).then_inc(r2_col, 1)
                dve.wait_ge(col_read, n_scale[0] + 1)
                if bound2 is None:
                    n_r2[0] += 1
                    dve.wait_ge(r2_all, n_r2[0])
                    step(dve.tensor_scalar(scl[:, 6:7], scl[:, 3:4], scl[:, 5:6], 4.0, ALU.mult, ALU.mult))
                else:
                    step(dve.tensor_scalar(scl[:, 6:7], scl[:, 3:4], float(bound2), None, ALU.mult))
                if bias_ap is not None:
                    step(dve.tensor_reduce(scl[:, 7:8], bias_ap, AX.X, ALU.max, apply_absolute_value=True))
                    step(dve.tensor_scalar(scl[:, 7:8], scl[:, 7:8], scl[:, 7:8], 4.0, ALU.mult, ALU.mult))
                    step(dve.tensor_tensor(scl[:, 6:7], scl[:, 6:7], scl[:, 7:8], ALU.add))
                step(dve.tensor_scalar(scl[:, 6:7], scl[:, 6:7], 1e-30, 1e38, ALU.max, ALU.min))
                step(dve.tensor_scalar(scl_i[:, 0:1], scl[:, 6:7].bitcast(I32), 23, None, ALU.logical_shift_right))
                step(dve.tensor_scalar(scl_i[:, 0:1], scl_i[:, 0:1], 1.0, None, ALU.add))
                step(dve.tensor_scalar(scl_i[:, 0:1], scl_i[:, 0:1], 1, None, ALU.logical_shift_right))
                step(dve.tensor_scalar(scl_i[:, 1:2], scl_i[:, 0:1], 49.0, None, ALU.add))
                step(dve.tensor_scalar(scl_i[:, 0:1], scl_i[:, 0:1], -1.0, 205.0, ALU.mult, ALU.add))
                dve.tensor_scalar(scl[:, 0:2].bitcast(I32), scl_i[:, 0:2], 23, None, ALU.logical_shift_left).then_inc(scale_ready, 1)
                n_scale[0] += 1
                dve.wait_ge(scale_ready, n_scale[0])

            n_r2, n_scale = [0], [0]

            def norm_end(n, i, k, st, y):
                kit = kits[k]
                dve.wait_ge(std_ready, tick(n, i))
                step(dve.reciprocal(st[:, 9:10], st[:, 8:9]))
                if tick(n, i) > 2:
                    t = NT * n + i
                    dve.wait_ge(y_out[i % 2], 16 * (t // 2))
                if n < 3 and i >= 2:
                    dve.wait_ge(t_ps, tick(R_OF[n], i - 2))
                dve.tensor_scalar(kit["yb"][:, i % 2, :], y, st[:, 6:7], st[:, 9:10], ALU.subtract, ALU.mult).then_inc(y_ready, 1)
                dve.wait_ge(y_ready, tick(n, i))

            dve.wait_ge(weights["wn"], 16)
            dve.wait_ge(x_sq, NT)
            dve.wait_ge(bb_in[0], 16)
            kit = kits[0]
            column_max(0, 1)
            scale(None, kit["bb"][:, 0, :])
            dve.wait_ge(gt_ps, 1)
            dve.tensor_copy(g_t.rearrange("p k r -> p (k r)"), psum[:, 3, 0:4 * RG]).then_inc(gt_ready, 1)
            for i in range(NT + 1):
                if i < NT:
                    dve.wait_ge(u_ps, i + 1)
                    if i >= 2:
                        dve.wait_ge(h1t_ps, i - 1)
                    dve.tensor_tensor(ua[:, i % 2, :], psum[:, 4 + i % 2, :], kit["bb"][:, 0, :], ALU.add).then_inc(h1_ready, 1)
                    dve.wait_ge(h1_ready, i + 1)
                    dve.tensor_scalar(hs[:, 0, 0, i, :], ua[:, i % 2, :], scl[:, 0:1], None, ALU.mult).then_inc(u_hi, 1)
                    dve.wait_ge(u_hi, i + 1)
                    dve.scalar_tensor_tensor(hs[:, 0, 1, i, :], ua[:, i % 2, :], scl[:, 0:1], hs[:, 0, 0, i, :], ALU.mult, ALU.subtract).then_inc(u_lo, 1)
                if i:
                    dve.wait_ge(h1t_ps, i)
                    dve.tensor_copy(xt[:, i - 1, :, :].rearrange("p k n -> p (k n)"), psum[:, 6, :]).then_inc(h1t_cp, 1)
            dve.wait_ge(g2_ps, 1)
            dve.tensor_copy(g2[0:RG, :], psum[0:RG, 0, :]).then_inc(g2_ready, 1)
            dve.wait_ge(bb_in[1], 16)
            for i in range(NT + 1):
                if i < NT:
                    dve.wait_ge(acc_ps, i + 1)
                    if i >= 2:
                        dve.wait_ge(m_ps, i - 1)
                    dve.scalar_tensor_tensor(ua[:, i % 2, :], psum[:, i % 2, :], scl[:, 1:2], kit["bb"][:, 1, :], ALU.mult, ALU.add).then_inc(acc_read, 1)
                    dve.wait_ge(m_ps, i + 1)
                    if i >= 2:
                        dve.wait_ge(o_ps, i - 1)
                    dve.tensor_copy(kit["mt"][:, i % 2, :, :].rearrange("p k n -> p (k n)"), psum[:, 6, :]).then_inc(m_cp, 1)
                if i:
                    j = i - 1
                    if j == 0:
                        dve.wait_ge(bb_in[0], 32)
                    dve.wait_ge(o_ps, j + 1)
                    dve.tensor_tensor(xt[:, j, :, :].rearrange("p k n -> p (k n)"), psum[:, 4 + j % 2, :], kit["bb"][:, 0, :], ALU.add).then_inc(o_read, 1)
            dve.wait_ge(tanh_used, 2 * RG)
            for c in range(3):
                dve.tensor_scalar(logit_t[:, 512 * c:512 * c + 512], psum[:, LOGIT[c], :], bcol[:, 4:5], None, ALU.add).then_inc(lt_ready, 1)
            dve.wait_ge(ln_ps, 1)
            logits = psum[:, 2:5, :].rearrange("p b c -> p (b c)").rearrange("p (i g c) -> p i g c", i=NT, g=4)[:, :, :, 0:9]
            step(dve.tensor_reduce(sm[:, 0, :], logits, AX.XY, ALU.max))
            for g in range(4):
                x = dve.tensor_tensor(att[:, :, 9 * g:9 * g + 9], logits[:, :, g, :], sm[:, 0, :].unsqueeze(2).broadcast_to([P, NT, 9]), ALU.subtract)
            x.then_inc(logit_ready, 1)
            dve.wait_ge(exp_ready, 1)
            step(dve.tensor_reduce(sm[:, 1, :], att, AX.X, ALU.add))
            step(dve.reciprocal(sm[:, 1, :], sm[:, 1, :]))
            dve.tensor_tensor(att, att, sm[:, 1, :].unsqueeze(2).broadcast_to([P, NT, RG]), ALU.mult).then_inc(att_ready, 1)
            dve.wait_ge(o_read, tick(0, NT - 1))
            for q in range(3):
                dve.wait_ge(att_ps, q + 1)
                dve.tensor_copy(att_t[0:RG, 512 * q:512 * q + 512], psum[0:RG, 4 + q, :]).then_inc(att_cp, 1)
            for j in range(NT):
                    v = kit["yb"][:, j % 2, :]
                    st = lnst[:, j % 2, :]
                    dve.wait_ge(seen_ps, j + 1)
                    if j >= 2:
                        dve.wait_ge(y_out[j % 2], 16 * (j // 2))
                        dve.wait_ge(t_ps, tick(0, j - 2))
                    dve.tensor_tensor(v, psum[:, j % 2, :], xt[:, j, :, :].rearrange("p k n -> p (k n)"), ALU.add).then_inc(seen_read, 1)
                    dve.wait_ge(seen_read, j + 1)
                    dve.wait_ge(res_in[j % 2], 16 * (j // 2 + 1))
                    step(dve.scalar_tensor_tensor(v, v, 0.0, kit["xin"][:, j % 2, :], ALU.max, ALU.add))
                    step(dve.bn_stats(st[:, 0:6], v))
                    dve.bn_aggr(st[:, 6:8], st[:, 0:6]).then_inc(var_ready, 1)
                    dve.wait_ge(std_ready, tick(0, j))
                    step(dve.reciprocal(st[:, 9:10], st[:, 8:9]))
                    dve.scalar_tensor_tensor(st[:, 10:11], st[:, 6:7], -1.0, st[:, 9:10], ALU.mult, ALU.mult).then_inc(norm_ready, 1)
                    next_column_max(j, 1)

            def layernorm(n, i, k, y):
                st = lnst[:, i % 2, :]
                step(dve.bn_stats(st[:, 0:6], y))
                dve.bn_aggr(st[:, 6:8], st[:, 0:6]).then_inc(var_ready, 1)
                norm_end(n, i, k, st, y)

            kit = kits[1]
            for l in range(2):
                r = 1 + l
                scale(520.0 if l == 0 else None)
                for i in range(NT):
                    dve.wait_ge(gate_sig, tick(l, i))
                    dve.tensor_scalar(gates[:, i % 2, 2:4], gates[:, i % 2, 0:2], scl[:, 0:1], None, ALU.mult).then_inc(gate_ready, 1)
                    dve.wait_ge(gate_ready, tick(l, i))
                    dve.wait_ge(u_hi, tick(r, i))
                    for t in range(2):
                        x = dve.scalar_tensor_tensor(hs[:, t, 1, i, :], psum[:, 2 + 2 * (i % 2) + t, :], gates[:, i % 2, 2 + t:3 + t],
                                                     hs[:, t, 0, i, :], ALU.mult, ALU.subtract)
                    x.then_inc(u_lo, 1)
                dve.wait_ge(bb_in[l], 16 * (3 if l == 0 else 2))
                for i in range(NT):
                    dve.wait_ge(o_ps, tick(r, i))
                    dve.tensor_tensor(vt[:, :], psum[:, 4 + i % 2, :], kit["bb"][:, l, :], ALU.add).then_inc(o_read, 1)
                    dve.wait_ge(o_read, tick(r, i))
                    dve.wait_ge(acc_ps, tick(r, i))
                    if l == 0:
                        if i >= 2:
                            dve.wait_ge(t_ps, tick(r, i - 2))
                            dve.wait_ge(v_ready, tick(0, i - 2))
                        dve.scalar_tensor_tensor(ua[:, i % 2, :], psum[:, i % 2, :], scl[:, 1:2], vt[:, :], ALU.mult, ALU.add).then_inc(acc_read, 1)
                        dve.wait_ge(acc_read, tick(r, i))
                        next_column_max(i, r + 1)
                    else:
                        dve.scalar_tensor_tensor(vt[:, :], psum[:, i % 2, :], scl[:, 1:2], vt[:, :], ALU.mult, ALU.add).then_inc(acc_read, 1)
                        dve.wait_ge(acc_read, tick(r, i))
                        t = NT + i
                        dve.wait_ge(res_in[i % 2], 16 * (t // 2 + 1))
                        step(dve.tensor_tensor(vt[:, :], vt[:, :], kit["xin"][:, i % 2, :], ALU.add))
                        layernorm(1, i, 1, vt[:, :])
                        next_column_max(i, r + 1)
                if l == 0:
                    dve.wait_ge(v_ready, tick(0, NT - 1))
            kit = kits[2]

            def log_softmax_end(i):
                v, st = kit["yb"][:, i % 2, :], lnst[:, i % 2, :]
                dve.wait_ge(lsm_exp, i + 1)
                step(dve.tensor_tensor(sml[:, i % 2, 3:4], sml[:, i % 2, 0:1], sml[:, i % 2, 2:3], ALU.subtract))
                dve.wait_ge(res_in[i % 2], 16 * ((2 * NT + i) // 2 + 1))
                dve.wait_ge(y_out[i % 2], 16 * ((2 * NT + i) // 2))
                if i >= 2:
                    dve.wait_ge(t_ps, tick(7, i - 2))
                step(dve.scalar_tensor_tensor(v, ua[:, i % 2, :], sml[:, i % 2, 3:4], kit["xin"][:, i % 2, :], ALU.add, ALU.add))
                step(dve.bn_stats(st[:, 0:6], v))
                dve.bn_aggr(st[:, 6:8], st[:, 0:6]).then_inc(var_ready, 1)

            def normed(i):
                v, st = kit["yb"][:, i % 2, :], lnst[:, i % 2, :]
                dve.wait_ge(std_ready, tick(2, i))
                step(dve.reciprocal(st[:, 9:10], st[:, 8:9]))
                dve.tensor_scalar(v, v, st[:, 6:7], st[:, 9:10], ALU.subtract, ALU.mult).then_inc(y_ready, 1)

            for l in range(5):
                r = 3 + l
                scale(520.0 if l == 0 else None)
                for i in range(NT):
                    dve.wait_ge(u_hi, tick(r, i))
                    step(dve.scalar_tensor_tensor(vt[:, :], psum[:, 2 + i % 2, :], scl[:, 0:1], hs[:, 0, 0, i, :], ALU.mult, ALU.subtract))
                    dve.tensor_scalar(hs[:, 0, 1, i, :], vt[:, :], LO_BY, None, ALU.mult).then_inc(u_lo, 1)
                    dve.wait_ge(u_lo, tick(r, i))
                dve.wait_ge(bb_in[r % 2], 16 * BB_COUNT[r])
                step(dve.tensor_scalar(scl[:, 2:3], epsc[:, l:l + 1], 1.0, None, ALU.add))
                for i in range(NT):
                    step(dve.scalar_tensor_tensor(vt[:, :], hs[:, 0, 1, i, :], 1.0 / LO_BY, hs[:, 0, 0, i, :], ALU.mult, ALU.add))
                    dve.wait_ge(acc_ps, tick(r, i))
                    step(dve.scalar_tensor_tensor(vt[:, :], vt[:, :], scl[:, 2:3], psum[:, i % 2, :], ALU.mult, ALU.add))
                    dve.scalar_tensor_tensor(vt[:, :], psum[:, 4 + i % 2, :], 1.0 / LO_BY, vt[:, :], ALU.mult, ALU.add).then_inc(acc_read, 1)
                    dve.wait_ge(acc_read, tick(r, i))
                    if i >= 2 and l < 4:
                        dve.wait_ge(t_ps, tick(r, i - 2))
                        dve.wait_ge(v_ready, tick(V_OF[r], i - 2))
                    dve.scalar_tensor_tensor(ua[:, i % 2, :], vt[:, :], scl[:, 1:2], kit["bb"][:, r % 2, :], ALU.mult, ALU.add).then_inc(v_pre, 1)
                    dve.wait_ge(v_pre, tick(V_OF[r] - 1, i))
                    if l == 4:
                        step(dve.tensor_scalar(ua[:, i % 2, :], ua[:, i % 2, :], 0.0, None, ALU.max))
                        dve.tensor_reduce(sml[:, i % 2, 0:1], ua[:, i % 2, :], AX.X, ALU.max, negate=True).then_inc(lsm_neg, 1)
                        if i >= 2:
                            normed(i - 2)
                        if i:
                            log_softmax_end(i - 1)
                    next_column_max(i, r + 1)
                if l == 4:
                    normed(NT - 2)
                    log_softmax_end(NT - 1)
                    normed(NT - 1)
                if l < 4:
                    dve.wait_ge(v_ready, tick(V_OF[r], NT - 1))
            dve.wait_ge(bb_in[0], 16 * BB_COUNT[8])
            for i in range(NT):
                dve.wait_ge(acc_ps, tick(8, i))
                dve.tensor_tensor(vt[:, :], psum[:, i % 2, :], kit["bb"][:, 0, :], ALU.add).then_inc(acc_read, 1)
                dve.wait_ge(acc_read, tick(8, i))
                t = 3 * NT + i
                dve.wait_ge(res_in[i % 2], 16 * (t // 2 + 1))
                step(dve.tensor_tensor(vt[:, :], vt[:, :], kit["xin"][:, i % 2, :], ALU.add))
                layernorm(3, i, 2, vt[:, :])

        @block.scalar
        def _(act):
            act.wait_ge(ranges_ready, 1)

            def side_lot(g, n, kind, a, q):
                bank = psum[:, 6 + n % 2, :]
                act.wait_ge(side_ps, side_at(g, n))
                if kind == "basis":
                    c = a * (CH // 2) + q
                    act.wait_ge(comb_out[c % 2], 64 * ((CH // 2) * g + c // 2 + 1))
                    act.activation(ua[:, c % 2, :], bank, ACT.Copy).then_inc(side_out, 1)
                elif q == 1:
                    for t in range(2):
                        x = act.activation(adj[:, 1 + t, bass.ds(g * BLOCKS + a, 1), (1 - t) * 1024:(1 - t) * 1024 + 512].rearrange("p o n -> p (o n)"),
                                           bank.bitcast(F16)[:, t * 512:t * 512 + 512], ACT.Copy)
                    x.then_inc(side_out, 1)
                elif q < 3:
                    act.activation(adj[:, 1 + q // 2, bass.ds(g * BLOCKS + a, 1), q // 2 * 512:q // 2 * 512 + 1024].rearrange("p o n -> p (o n)"),
                                   bank.bitcast(F16), ACT.Copy).then_inc(side_out, 1)
                else:
                    if q == 3:
                        act.wait_ge(row_out, 16 * (BLOCKS * g + a + 1))
                    act.activation(aw_row[:, 512 * (q - 3):512 * (q - 2)], bank, ACT.Copy).then_inc(side_out, 1)
                    if q == 5:
                        act.wait_ge(side_out, side_copied(g, n))
                        act.dma_start(aw_dram[:, bass.ds(g * BLOCKS + a, 1), :].rearrange("p o n -> p (o n)"), aw_row).then_inc(row_out, 16)

            with act.Fori(0, NB) as g:
                following = act.value_load(wrow_i[0:1, 2, bass.ds(g * GB, 1)], min_val=1, max_val=NW * MOST)
                for u in range(GB):
                    w = g * GB + u
                    b, s = u % 2, u // 8
                    through = following
                    if u + 1 < GB:
                        following = act.value_load(wrow_i[0:1, 2, bass.ds(w + 1, 1)], min_val=1, max_val=NW * MOST)
                    act.wait_ge(onehot_free[STEP - 1], through + 1)
                    act.activation(adj[:, 0, :, bass.ds(w * W, W)], win[b][:, :, 0:W], ACT.Copy)
                    if u % 8 == 0:
                        act.wait_ge(side_ps, stage_free_at(g, s))
                    act.activation(typed[:, s % 2, :, :, W * (u % 8):W * (u % 8) + W].rearrange("p m j d -> p j m d"),
                                   win[b][:, :, W:3 * W].rearrange("p j (m d) -> p j m d", m=2), ACT.Copy)
                    act.wait_ge(wparts_free[b], HB * g + u // 2 + 1)
                    act.activation(wparts[:, b, :, :], win[b][:, :, 3 * W:6 * W], ACT.Copy).then_inc(win_free[b], 1)
                    for lot in by_window[u]:
                        side_lot(g, *lot)

            act.drain().then_inc(built, 1)

            n_act = [0]

            def step(ins_):
                n_act[0] += 1
                ins_.then_inc(act_done, 1)
                act.wait_ge(act_done, n_act[0])

            act.wait_ge(built, 4)
            for k in range(2):
                act.wait_ge(comb_out[k], 64 * 33)
            for i in range(NT):
                act.wait_ge(x_in[i // 3], 16)
                if i == 3:
                    act.dma_start(img[0:RG, :], ins["L0_gnn_img_feats"][0]).then_inc(weights["img"], 16)
                    act.dma_start(wi, ins["L0_gnn_Wi"].rearrange("(k p) n -> p k n", p=P)).then_inc(weights["wi"], 16)
                if i == 9:
                    act.dma_start(wb[:, 1, :, :], ins["L0_gnn_Wn"].rearrange("(k p) n -> p k n", p=P)).then_inc(weights["wn"], 16)
                    act.dma_start(wim, ins["L0_gnn_Wim"].rearrange("(k p) n -> p k n", p=P)).then_inc(weights["wim"], 16)
                if i >= 2:
                    act.wait_ge(x_sq, i - 1)
                act.activation(ua[:, i % 2, :], x_first[:, i % 9, :], ACT.Square, accum_out=norm2[:, i:i + 1]).then_inc(x_sq, 1)

            seen = [0]

            def colnorms(slot, chunks, squares):
                for c in chunks:
                    seen[0] += 1
                    if seen[0] > 2:
                        act.wait_ge(sq_used, seen[0] - 2)
                    act.activation(squares[:, c % 2, :], wb[:, slot + c // 4, c % 4, :], ACT.Square).then_inc(sq_ready, 1)

            def next_colnorms(r, i):
                c = 2 * (i - 5)
                if 0 <= c < CHUNKS_OF[r]:
                    if c == 0:
                        act.wait_ge(weights["l1" + "ab"[r - 1]] if r < 3 else gin_in[r - 3], 32 if r < 3 else 16)
                    colnorms(0 if r < 3 else r % 2, (c, c + 1), squares_of(r))

            act.wait_ge(weights["wn"], 16)
            act.wait_ge(x_sq, NT)
            colnorms(1, range(4), ua)
            act.wait_ge(pb_ready, 1)
            act.wait_ge(proj_cp, 6)
            act.wait_ge(weights["ts_out"], 16)
            for n in range(2 * RG):
                h, r = n // 4 % 2, 9 * (n % 4) + n // 8
                if n >= 3:
                    act.wait_ge(tanh_used, n - 2)
                act.activation(tanh[:, n % 3, :], proj[:, h, :], ACT.Tanh, bias=pbias[:, h, r:r + 1]).then_inc(tanh_ready, 1)
            act.wait_ge(logit_ready, 1)
            act.activation(att, att, ACT.Exp).then_inc(exp_ready, 1)
            for i in range(NT + 1):
                if i < NT:
                    y, st = kits[0]["yb"][:, i % 2, :], lnst[:, i % 2, :]
                    act.wait_ge(var_ready, tick(0, i))
                    act.activation(st[:, 8:9], st[:, 7:8], ACT.Sqrt, bias=bcol[:, 5:6]).then_inc(std_ready, 1)
                    act.wait_ge(norm_ready, i + 1)
                    act.activation(y, y, ACT.Identity, bias=st[:, 10:11], scale=st[:, 9:10]).then_inc(y_ready, 1)
                if i == 0:
                    continue
                j = i - 1
                act.wait_ge(t_ps, tick(0, j))
                act.activation(xt[:, j, :, :].rearrange("p k n -> p (k n)"), psum[:, 7, :], ACT.Copy).then_inc(t_cp, 1)
                next_colnorms(1, j)

            def transposed(r, i):
                act.wait_ge(t_ps, tick(r, i))
                act.activation(xt[:, i, :, :].rearrange("p k n -> p (k n)"), psum[:, 7, :], ACT.Copy).then_inc(t_cp, 1)
                next_colnorms(r + 1, i)

            def std(n, i):
                act.wait_ge(var_ready, tick(n, i))
                act.activation(lnst[:, i % 2, 8:9], lnst[:, i % 2, 7:8], ACT.Sqrt, bias=bcol[:, 5:6]).then_inc(std_ready, 1)

            def relu(r, i):
                if r == 1:
                    act.wait_ge(acc_read, tick(r, i))
                else:
                    act.wait_ge(v_pre, tick(V_OF[r] - 1, i))
                act.activation(ua[:, i % 2, :], ua[:, i % 2, :], ACT.Relu).then_inc(relu_ready, 1)
                act.wait_ge(relu_ready, tick(V_OF[r], i))
                act.activation(kits[kit_of[r]]["mt"][:, i % 2, :, :].rearrange("p k n -> p (k n)"), ua[:, i % 2, :], ACT.Square,
                               accum_out=norm2[:, i:i + 1]).then_inc(v_ready, 1)

            for l in range(2):
                r = 1 + l
                act.wait_ge(scale_ready, 2 + l)
                for i in range(NT):
                    act.wait_ge(gate_ps, tick(l, i))
                    if i >= 2:
                        act.wait_ge(u_lo, tick(r, i - 2))
                    act.activation(gates[:, i % 2, 0:2], psum[:, 6 + i % 2, 0:2], ACT.Sigmoid).then_inc(gate_sig, 1)
                    act.wait_ge(gate_ready, tick(l, i))
                    act.wait_ge(u_ps, tick(r, i))
                    for t in range(2):
                        x = act.activation(hs[:, t, 0, i, :], psum[:, 2 + 2 * (i % 2) + t, :], ACT.Copy, scale=gates[:, i % 2, 2 + t:3 + t])
                    x.then_inc(u_hi, 1)
                for i in range(NT + 1):
                    if l == 0:
                        if i < NT:
                            relu(r, i)
                    elif i < NT:
                        std(1, i)
                    if i:
                        transposed(r, i - 1)
            for l in range(5):
                r = 3 + l
                act.wait_ge(scale_ready, 4 + l)
                for i in range(NT):
                    act.wait_ge(u_ps, tick(r, i))
                    act.activation(hs[:, 0, 0, i, :], psum[:, 2 + i % 2, :], ACT.Copy, scale=scl[:, 0:1]).then_inc(u_hi, 1)
                for i in range(NT + 1):
                    if i < NT:
                        if l < 4:
                            relu(r, i)
                        else:
                            act.wait_ge(lsm_neg, i + 1)
                            step(act.activation(kits[2]["mt"][:, i % 2, :, :].rearrange("p k n -> p (k n)"), ua[:, i % 2, :], ACT.Exp,
                                                bias=sml[:, i % 2, 0:1], accum_out=sml[:, i % 2, 1:2]))
                            act.activation(sml[:, i % 2, 2:3], sml[:, i % 2, 1:2], ACT.Ln).then_inc(lsm_exp, 1)
                            if i:
                                std(2, i - 1)
                    if l == 4 and i == NT:
                        std(2, i - 1)
                    if l == 4 and i >= 3:
                        transposed(r, i - 3)
                    if l < 4 and i:
                        transposed(r, i - 1)
                if l == 4:
                    transposed(r, NT - 2)
                    transposed(r, NT - 1)
            for i in range(NT):
                act.wait_ge(u_ps, tick(8, i))
                act.activation(sup[:, i, :], psum[:, 2 + i % 2, :], ACT.Copy).then_inc(u_hi, 1)
            for i in range(NT):
                std(3, i)

        @block.tensor
        def _(pe):
            pe.wait_ge(c_ready, 7)
            pe.wait_ge(edges_in, 64)
            pe.wait_ge(erow_ready, 1)
            for a in range(4):
                for h in range(2):
                    c = 256 * (a % 2) + ER * h
                    x = pe.transpose(psum[:, a // 2, c:c + ER], erow[0:ER, a, P * h:P * h + P], ident[0:ER, 0:ER])
            x.then_inc(ecol_ps, 1)
            pe.wait_ge(span_ready, 4)
            for f in range(2):
                for h in range(2):
                    x = pe.transpose(psum[0:NW, 2 + f, ER * h:ER * h + ER], span[0:ER, f, h, :], ident[0:ER, 0:ER])
            x.then_inc(spant_ps, 1)
            pe.wait_ge(wcol_ready, 1)
            for f in range(2):
                x = pe.matmul(psum[0:1, 4, NW * f:NW * f + NW], wcol[0:NW, 2 + f:3 + f], ident[0:NW, 0:NW], start=True, stop=True)
            x.then_inc(wrow_ps, 1)
            pe.wait_ge(ranges_ready, 1)
            pe.wait_ge(attw_ready, 2)

            def side_lot(g, n, kind, a, q):
                bank = psum[:, 6 + n % 2, :]
                pe.wait_ge(side_out, side_copied(g, n - 2))
                if kind == "basis":
                    c = a * (CH // 2) + q
                    pe.wait_ge(basis_in[c % 2], 16 * ((CH // 2) * g + c // 2 + 1))
                    for v in range(4):
                        x = pe.matmul(bank[32 * v:32 * v + 32, :], attw[0:120, a, :], basis[c % 2][0:120, D * v:D * v + D], start=True, stop=True)
                else:
                    if q == 0:
                        for k in range(2):
                            pe.wait_ge(wparts_free[k], HB * g + 4 * a + 5)
                    if q < 3:
                        for m in range(8):
                            t, j = divmod(8 * q + m, NT)
                            x = pe.transpose(bank.bitcast(F16)[:, P * m:P * m + P], typed[:, a % 2, t, j, :], ident16[:])
                    else:
                        for m in range(4):
                            x = pe.transpose(bank[:, P * m:P * m + P], aw_stage[:, a % 2, 4 * (q - 3) + m, :], ident[:])
                x.then_inc(side_ps, 1)

            def window(w):
                return pe.value_load(wrow_i[0:1, 0, bass.ds(w, 1)], min_val=0, max_val=PACKED)

            with pe.Fori(0, NB) as g:
                following = window(g * GB)
                for u in range(GB):
                    w = g * GB + u
                    b = u % 2
                    _, steps, before = unpack(following)
                    if u + 1 < GB:
                        following = window(w + 1)
                    pe.wait_ge(win_free[b], HB * g + u // 2 + 1)
                    for j in range(0, NT, 4):
                        pe.matmul(win[b][:, j, 0:2], zeros, zeros[:, 0:2], start=True, stop=True, skip_group_check=True)
                    with pe.Fori(0, steps) as q:
                        for k in range(STEP):
                            pe.wait_ge(onehot_ready[k], before + q + 1)
                            for j in range(NT):
                                x = pe.matmul(win[b][:, j, 0:NPART * W], onehot_s[:, k, P * j:P * j + P],
                                              onehot_d[:, k, :, :].rearrange("p v w -> p (v w)"), start=False, stop=True, skip_group_check=True)
                            x.then_inc(onehot_free[k], 1)
                    for lot in by_window[u]:
                        side_lot(g, *lot)
            pe.drain().then_inc(built, 1)

            pe.wait_ge(built, 4)
            def x_turned(tiles):
                for i in tiles:
                    pe.wait_ge(x_in[i // 3], 16)
                    if i >= 2:
                        pe.wait_ge(x_cp, i - 1)
                    for k in range(4):
                        x = pe.transpose(psum[:, 6 + i % 2, P * k:P * k + P], x_first[:, i % 9, P * k:P * k + P], ident[:])
                    x.then_inc(x_ps, 1)

            x_turned(range(9))
            pe.wait_ge(weights["img"], 16)
            for k in range(8):
                x = pe.transpose(psum[:, 4, RG * k:RG * k + RG], img[0:RG, P * k:P * k + P], ident[0:RG, 0:RG])
            x.then_inc(imgt_ps, 1)
            pe.wait_ge(imgt_cp, 1)
            pe.wait_ge(weights["wi"], 16)
            for h in range(2):
                for k in range(8):
                    x = pe.matmul(psum[:, 5, RG * h:RG * h + RG], wi[:, k, P * h:P * h + P], img_t[:, k, :], start=k == 0, stop=k == 7)
            x.then_inc(ip_ps, 1)
            x_turned(range(9, NT))
            pe.wait_ge(x_cp, NT)
            pe.wait_ge(weights["wf"], 16)
            for q in range(6):
                h, c = q % 2, q // 2
                if q >= 2:
                    pe.wait_ge(proj_cp, q - 1)
                for k in range(4):
                    x = pe.matmul(psum[:, 6 + q % 2, :].rearrange("p (a n) -> p a n", a=4), wf[:, k, P * h:P * h + P], xt[:, 4 * c:4 * c + 4, k, :], start=k == 0, stop=k == 3)
                x.then_inc(proj_ps, 1)
            seen = [0]

            def colnorms(bank, chunks, squares):
                for c in chunks:
                    seen[0] += 1
                    pe.wait_ge(sq_ready, seen[0])
                    pe.matmul(psum[:, bank + c // 4, :], ones[:], squares[:, c % 2, :], start=c % 4 == 0, stop=c % 4 == 3).then_inc(sq_used, 1)

            def rows(bank, i, w, first=True, last=True):
                for k in range(4):
                    x = pe.matmul(psum[:, bank, :], xt[:, i, k, :], w[:, k, :], start=first and k == 0, stop=last and k == 3)
                return x

            def aggregate(r, i, mats, between=None):
                n = 0
                for t, m in enumerate(mats):
                    for j in range(NT):
                        if i == 0 and t == 0:
                            pe.wait_ge(u_hi, tick(r, j))
                            pe.wait_ge(u_lo, tick(r, j))
                        for half in range(2):
                            n += 1
                            own = r in range(3, 8)
                            x = pe.matmul(psum[:, i % 2 + (4 * half if own else 0), :], adj[:, m, j, P * i:P * i + P], hs[:, t, half, j, :],
                                          start=n == 1 or (own and n == 2), stop=n == 2 * NT * len(mats) or (own and n == 2 * NT - 1))
                        if n == 2 * NT * len(mats):
                            x.then_inc(acc_ps, 1)
                        if between and j % 3 == 2:
                            between(1)

            def back(i):
                for k in range(4):
                    x = pe.transpose(psum[:, 7, P * k:P * k + P], src_t(i)[:, P * k:P * k + P], ident[:])
                return x

            def next_colnorms(r, i):
                c = 2 * (i - 6)
                if 0 <= c < CHUNKS_OF[r]:
                    colnorms(2, (c, c + 1), squares_of(r))

            def u_tile(r, i):
                pe.wait_ge(t_cp, tick(r - 1, i))
                if i == 0:
                    pe.wait_ge(col_read, min(r + 1, 8))
                if i == 1 and r <= 2:
                    pe.wait_ge(t_cp, tick(r - 1, NT - 1))
                    pe.wait_ge(acc_read, tick(r - 1, NT - 1))
                if r in (1, 2):
                    l = r - 1
                    if i >= 2:
                        pe.wait_ge(u_lo, tick(r, i - 2))
                        pe.wait_ge(gate_sig, tick(l, i - 2))
                    for k in range(4):
                        x = pe.matmul(psum[:, 6 + i % 2, 0:2], xt[:, i, k, :], gw[:, l, k, :], start=k == 0, stop=k == 3)
                    x.then_inc(gate_ps, 1)
                    b = 2 + 2 * (i % 2)
                    rows(b, i, wb[:, 0, :, :])
                    rows(b + 1, i, wb[:, 1, :, :]).then_inc(u_ps, 1)
                else:
                    if i == 0:
                        pe.wait_ge(gin_in[r - 3], 16)
                    if i >= 2:
                        pe.wait_ge(u_lo if r < 8 else u_hi, tick(r, i - 2))
                    rows(2 + i % 2, i, wb[:, r % 2, :, :]).then_inc(u_ps, 1)

            n_dots = [0]

            def dots(count):
                for _ in range(count):
                    n = n_dots[0]
                    n_dots[0] += 1
                    a, h, g = n // 8, n // 4 % 2, n % 4
                    pe.wait_ge(tanh_ready, n + 1)
                    for c in range(3):
                        x = pe.matmul(psum[32 * g:32 * g + 32, LOGIT[c], :], wa_pad[:, h, 31 - a:63 - a], tanh[:, n % 3, 512 * c:512 * c + 512],
                                      start=a == 0 and h == 0, stop=a == 8 and h == 1)
                    x.then_inc(tanh_used, 1)

            pe.wait_ge(weights["wn"], 16)
            colnorms(0, range(4), ua)
            pe.wait_ge(weights["wim"], 16)
            for k in range(4):
                for c in range(8):
                    x = pe.matmul(psum[:, 3, RG * k:RG * k + RG], wim[:, c, P * k:P * k + P], img_t[:, c, :], start=c == 0, stop=c == 7)
            x.then_inc(gt_ps, 1)
            pe.wait_ge(gt_ready, 1)
            for i in range(NT + 1):
                if i < NT:
                    if i >= 2:
                        pe.wait_ge(h1_ready, i - 1)
                    rows(4 + i % 2, i, wb[:, 1, :, :]).then_inc(u_ps, 1)
                    dots(1)
                if i > 0:
                    pe.wait_ge(h1_ready, i)
                    if i > 1:
                        pe.wait_ge(h1t_cp, i - 1)
                    for k in range(4):
                        x = pe.transpose(psum[:, 6, P * k:P * k + P], ua[:, (i - 1) % 2, P * k:P * k + P], ident[:])
                    x.then_inc(h1t_ps, 1)
            pe.wait_ge(weights["wt"], 16)
            for k in range(4):
                x = pe.matmul(psum[0:RG, 0, :], g_t[:, k, :], wb[:, 0, k, :], start=k == 0, stop=k == 3)
            x.then_inc(g2_ps, 1)
            pe.wait_ge(g2_ready, 1)
            pe.wait_ge(weights["wbm"], 16)
            pe.wait_ge(h1t_cp, NT)
            for i in range(NT + 1):
                if i < NT:
                    if i >= 2:
                        pe.wait_ge(acc_read, tick(0, i - 2))
                    aggregate(0, i, [0], between=dots)
                if i:
                    j = i - 1
                    pe.wait_ge(acc_read, tick(0, j))
                    if j:
                        pe.wait_ge(m_cp, j)
                    for k in range(4):
                        x = pe.transpose(psum[:, 6, P * k:P * k + P], ua[:, j % 2, P * k:P * k + P], ident[:])
                    x.then_inc(m_ps, 1)
                    dots(1)
                    if j >= 2:
                        pe.wait_ge(o_read, tick(0, j - 2))
                    rows(4 + j % 2, j, wb[:, 1, :, :], last=False)
                    pe.wait_ge(m_cp, j + 1)
                    for k in range(4):
                        x = pe.matmul(psum[:, 4 + j % 2, :], kits[0]["mt"][:, j % 2, k, :], wb[:, 0, k, :], start=False, stop=k == 3)
                    x.then_inc(o_ps, 1)
            pe.wait_ge(lt_ready, 3)
            pe.wait_ge(o_read, tick(0, NT - 1))
            for i in range(NT):
                x = pe.transpose(psum[:, 2 + i // 4, P * (i % 4):P * (i % 4) + P], logit_t[:, P * i:P * i + P], ident[:])
            x.then_inc(ln_ps, 1)
            pe.wait_ge(att_ready, 1)
            for q in range(3):
                for k in range(4):
                    x = pe.transpose(psum[0:RG, 4 + q, P * k:P * k + P], att[:, 4 * q + k, :], ident[:])
                x.then_inc(att_ps, 1)

            def attended(j):
                pe.wait_ge(att_cp, j // 4 + 1)
                if j >= 2:
                    pe.wait_ge(seen_read, j - 1)
                pe.matmul(psum[:, j % 2, :], att_t[0:RG, P * j:P * j + P], g2[0:RG, :], start=True, stop=True).then_inc(seen_ps, 1)

            attended(0)
            attended(1)
            for j in range(NT):
                if j + 2 < NT:
                    attended(j + 2)
                if j == NT - 1:
                    pe.wait_ge(att_cp, 3)
                    u_tile(1, 0)
                pe.wait_ge(y_ready, tick(0, j))
                if j:
                    pe.wait_ge(t_cp, tick(0, j - 1))
                for k in range(4):
                    x = pe.transpose(psum[:, 7, P * k:P * k + P], kits[0]["yb"][:, j % 2, P * k:P * k + P], ident[:])
                x.then_inc(t_ps, 1)
                next_colnorms(1, j)

            def finish(r, i, src, ready):
                if i == NT - 1:
                    u_tile(r + 1, 0)
                    if r >= 2:
                        u_tile(r + 1, 1)
                pe.wait_ge(ready, tick(V_OF[r] if ready is relu_ready else NORM_OF[r], i))
                if i:
                    pe.wait_ge(t_cp, tick(r, i - 1))
                for k in range(4):
                    x = pe.transpose(psum[:, 7, P * k:P * k + P], src[:, i % 2, P * k:P * k + P], ident[:])
                x.then_inc(t_ps, 1)
                next_colnorms(r + 1, i)

            for l in range(2):
                r = 1 + l
                for i in range(1, NT):
                    u_tile(r, i)
                if l == 0:
                    pe.wait_ge(weights["ts_in"], 16)
                pe.wait_ge(weights["root"], 16 * (l + 1))
                src, ready = (ua, relu_ready) if l == 0 else (kits[1]["yb"], y_ready)
                for i in range(NT + 1):
                    if i < NT:
                        pe.wait_ge(acc_read, tick(r, i - 2))
                        aggregate(r, i, [1, 2])
                        if i < 2:
                            pe.wait_ge(u_lo, tick(r, NT - 1))
                        pe.wait_ge(o_read, tick(r, i - 2))
                        rows(4 + i % 2, i, root).then_inc(o_ps, 1)
                    if i:
                        finish(r, i - 1, src, ready)
            for l in range(5):
                r = 3 + l
                for i in range(2, NT):
                    u_tile(r, i)
                if l == 0:
                    pe.wait_ge(weights["as_in"], 16)
                src, ready = (ua, relu_ready) if l < 4 else (kits[2]["yb"], y_ready)
                late = 3 if l == 4 else 1
                for i in range(NT + late):
                    if i < NT:
                        pe.wait_ge(acc_read, tick(r, i - 2))
                        aggregate(r, i, [0])
                    if i >= late:
                        finish(r, i - late, src, ready)
            r = 8
            for i in range(2, NT):
                u_tile(r, i)
            pe.wait_ge(weights["aw"], 16)
            for i in range(NT):
                pe.wait_ge(acc_read, tick(r, i - 2))
                for j in range(NT):
                    if i == 0:
                        pe.wait_ge(u_hi, tick(r, j))
                    x = pe.matmul(psum[:, i % 2, :], aw[:, j, P * i:P * i + P], sup[:, j, :], start=j == 0, stop=j == NT - 1)
                x.then_inc(acc_ps, 1)


def kernel(**inputs):
    import numpy as np
    import concourse.bacc as bacc
    from concourse.bass_utils import run_bass_kernel_spmd

    nc = bacc.Bacc("TRN2", target_bir_lowering=False, num_devices=1)
    arrays, aps = {}, {}
    for name, a in inputs.items():
        a = np.ascontiguousarray(a)
        arrays[f"in_{name}"] = a
        aps[name] = nc.dram_tensor(f"in_{name}", a.shape, mybir.dt.from_np(a.dtype), kind="ExternalInput").ap()
    out = nc.dram_tensor("out", [N, D], F32, kind="ExternalOutput").ap()
    program(nc, aps, out)
    r = run_bass_kernel_spmd(nc, [arrays], core_ids=[0])
    return r.results[0]["out"]
```
